# Optimizing a Trainium2 kernel written in Bass

```python
import numpy as np
import jax
import jax.numpy as jnp

def _softmax(x, axis=-1):
    return jax.nn.softmax(x, axis=axis)

def _gelu(x):
    return jax.nn.gelu(x, approximate=True)

def _silu(x):
    return jax.nn.silu(x)

def _sigmoid(x):
    return jax.nn.sigmoid(x)

def _layernorm(x, axis=-1, eps=1e-05):
    m = jnp.mean(x, axis=axis, keepdims=True)
    v = jnp.var(x, axis=axis, keepdims=True)
    return (x - m) / jnp.sqrt(v + eps)

def _scatter_add(tgt, idx, src, axis=0):
    return tgt.at[idx].add(src)

def _segment_sum(src, seg, n):
    return jax.ops.segment_sum(src, seg, n)
kernel_name = 'mk_conv_preact_d2_conv_nhwc768_r2_1bedc6'

def setup_inputs(seed: int=0):
    np.random.seed(seed)
    _w = jnp.asarray

    def _rec_inputs():
        import jax
        import jax.numpy as jnp
        _gk = jax.random.key(seed)
        x = -0.0005058 + 1 * jax.random.normal(jax.random.fold_in(_gk, 1), (2, 48, 48, 384), jnp.float32)
        return x
    x = _rec_inputs()

    def _L0_conv_setup():
        import jax, jax.numpy as jnp
        import numpy as np
        D_MODEL = 384
        D_HEAD = 32
        N_HEADS = D_MODEL // D_HEAD
        KERNEL = 7
        NEG_INF = -1e+30

        def make_neighbourhood_mask(kernel_h, kernel_w, canvas_h, canvas_w):
            h_ramp = jnp.arange(canvas_h)
            w_ramp = jnp.arange(canvas_w)
            h_pos, w_pos = jnp.meshgrid(h_ramp, w_ramp, indexing='ij')
            start_h = jnp.clip(h_pos - kernel_h // 2, 0, canvas_h - kernel_h)[..., None, None]
            end_h = start_h + kernel_h
            start_w = jnp.clip(w_pos - kernel_w // 2, 0, canvas_w - kernel_w)[..., None, None]
            end_w = start_w + kernel_w
            h_range = h_ramp.reshape(1, 1, canvas_h, 1)
            w_range = w_ramp.reshape(1, 1, 1, canvas_w)
            mask = (h_range >= start_h) & (h_range < end_h) & (w_range >= start_w) & (w_range < end_w)
            return mask.reshape(canvas_h * canvas_w, canvas_h * canvas_w)
        key = jax.random.key(seed)
        k1, k2, k3, k4, k5, k6 = jax.random.split(key, 6)
        x = jax.random.normal(k1, (2, 48, 48, D_MODEL), dtype=jnp.float32)
        registers = jax.random.normal(k2, (16, D_MODEL), dtype=jnp.float32)
        scale = 1.0 / np.sqrt(D_MODEL)
        qkv_w = jax.random.normal(k3, (3 * D_MODEL, D_MODEL), dtype=jnp.float32) * scale
        qkv_b = jax.random.normal(k4, (3 * D_MODEL,), dtype=jnp.float32) * 0.01
        out_w = jax.random.normal(k5, (D_MODEL, D_MODEL), dtype=jnp.float32) * scale
        out_b = jax.random.normal(k6, (D_MODEL,), dtype=jnp.float32) * 0.01
        return {'x': x, 'registers': registers, 'qkv_w': qkv_w, 'qkv_b': qkv_b, 'out_w': out_w, 'out_b': out_b}
    _L0_conv_all = _L0_conv_setup()
    _L0_conv_in = {k: v for k, v in _L0_conv_all.items() if k in ('registers', 'qkv_w', 'qkv_b', 'out_w', 'out_b')}
    del _L0_conv_all

    def _L1_conv_setup():
        import jax, jax.numpy as jnp
        import numpy as np
        B, H, W, C = (32, 32, 32, 384)
        E = 4
        TOPK = 2
        HD = int(C * 0.25)
        key = jax.random.key(seed)
        ks = jax.random.split(key, 7)
        x = jax.random.normal(ks[0], (B, H, W, C), dtype=jnp.float32)
        router_w = jax.random.normal(ks[1], (E, C), dtype=jnp.float32) * 0.02
        router_b = jnp.zeros((E,), dtype=jnp.float32)
        fc1_w = jax.random.normal(ks[2], (E, HD, C), dtype=jnp.float32) * (1.0 / np.sqrt(C))
        fc1_b = jax.random.normal(ks[3], (E, HD), dtype=jnp.float32) * 0.01
        fc2_w = jax.random.normal(ks[4], (E, C, HD), dtype=jnp.float32) * (1.0 / np.sqrt(HD))
        fc2_b = jax.random.normal(ks[5], (E, C), dtype=jnp.float32) * 0.01
        return {'x': x, 'router_w': router_w, 'router_b': router_b, 'fc1_w': fc1_w, 'fc1_b': fc1_b, 'fc2_w': fc2_w, 'fc2_b': fc2_b}
    _L1_conv_all = _L1_conv_setup()
    _L1_conv_in = {k: v for k, v in _L1_conv_all.items() if k in ('router_w', 'router_b', 'fc1_w', 'fc1_b', 'fc2_w', 'fc2_b')}
    del _L1_conv_all
    return {'x': x, 'L0_conv_registers': _L0_conv_in['registers'], 'L0_conv_qkv_w': _L0_conv_in['qkv_w'], 'L0_conv_qkv_b': _L0_conv_in['qkv_b'], 'L0_conv_out_w': _L0_conv_in['out_w'], 'L0_conv_out_b': _L0_conv_in['out_b'], 'L1_conv_router_w': _L1_conv_in['router_w'], 'L1_conv_router_b': _L1_conv_in['router_b'], 'L1_conv_fc1_w': _L1_conv_in['fc1_w'], 'L1_conv_fc1_b': _L1_conv_in['fc1_b'], 'L1_conv_fc2_w': _L1_conv_in['fc2_w'], 'L1_conv_fc2_b': _L1_conv_in['fc2_b']}

def reference(x, L0_conv_registers, L0_conv_qkv_w, L0_conv_qkv_b, L0_conv_out_w, L0_conv_out_b, L1_conv_router_w, L1_conv_router_b, L1_conv_fc1_w, L1_conv_fc1_b, L1_conv_fc2_w, L1_conv_fc2_b):
    import jax
    import jax.numpy as jnp

    def _L0_conv_ref(x, registers, qkv_w, qkv_b, out_w, out_b):
        import jax, jax.numpy as jnp
        import numpy as np
        D_MODEL = 384
        D_HEAD = 32
        N_HEADS = D_MODEL // D_HEAD
        KERNEL = 7
        NEG_INF = -1e+30

        def make_neighbourhood_mask(kernel_h, kernel_w, canvas_h, canvas_w):
            h_ramp = jnp.arange(canvas_h)
            w_ramp = jnp.arange(canvas_w)
            h_pos, w_pos = jnp.meshgrid(h_ramp, w_ramp, indexing='ij')
            start_h = jnp.clip(h_pos - kernel_h // 2, 0, canvas_h - kernel_h)[..., None, None]
            end_h = start_h + kernel_h
            start_w = jnp.clip(w_pos - kernel_w // 2, 0, canvas_w - kernel_w)[..., None, None]
            end_w = start_w + kernel_w
            h_range = h_ramp.reshape(1, 1, canvas_h, 1)
            w_range = w_ramp.reshape(1, 1, 1, canvas_w)
            mask = (h_range >= start_h) & (h_range < end_h) & (w_range >= start_w) & (w_range < end_w)
            return mask.reshape(canvas_h * canvas_w, canvas_h * canvas_w)
        n, h, w, _ = x.shape
        nh, e = (N_HEADS, D_HEAD)
        s = h * w
        r = registers.shape[0]
        qkv = x @ qkv_w.T + qkv_b
        qkv = qkv.reshape(n, h, w, 3, nh, e)
        qkv = qkv.transpose(3, 0, 4, 1, 2, 5).reshape(3, n, nh, s, e)
        q, k, v = (qkv[0], qkv[1], qkv[2])
        reg_kv = registers @ qkv_w[D_MODEL:].T + qkv_b[D_MODEL:]
        reg_kv = reg_kv.reshape(r, 2, nh, e).transpose(1, 2, 0, 3)
        reg_k = jnp.broadcast_to(reg_kv[0][None], (n, nh, r, e))
        reg_v = jnp.broadcast_to(reg_kv[1][None], (n, nh, r, e))
        k_cat = jnp.concatenate([k, reg_k], axis=-2)
        v_cat = jnp.concatenate([v, reg_v], axis=-2)
        mask = make_neighbourhood_mask(KERNEL, KERNEL, h, w)
        mask_cat = jnp.concatenate([mask, jnp.ones((s, r), dtype=bool)], axis=-1)
        scale = 1.0 / jnp.sqrt(jnp.asarray(e, dtype=x.dtype))
        scores = jnp.einsum('bnqe,bnke->bnqk', q, k_cat) * scale
        scores = jnp.where(mask_cat[None, None], scores, NEG_INF)
        attn = jax.nn.softmax(scores, axis=-1)
        o = jnp.einsum('bnqk,bnke->bnqe', attn, v_cat)
        o = o.transpose(0, 2, 1, 3).reshape(n, h, w, nh * e)
        return o @ out_w.T + out_b

    def _L1_conv_ref(x, router_w, router_b, fc1_w, fc1_b, fc2_w, fc2_b):
        import jax, jax.numpy as jnp
        import numpy as np
        B, H, W, C = (32, 32, 32, 384)
        E = 4
        TOPK = 2
        HD = int(C * 0.25)
        b, h, w, c = x.shape
        xt = x.reshape(b, h * w, c)
        logits = jnp.einsum('bsc,ec->bse', xt, router_w) + router_b
        probs = jax.nn.softmax(logits, axis=-1)
        topk_w, topk_idx = jax.lax.top_k(probs, TOPK)
        topk_w = topk_w / (jnp.sum(topk_w, axis=-1, keepdims=True) + 1e-08)
        combine = jnp.sum(jax.nn.one_hot(topk_idx, E, dtype=xt.dtype) * topk_w[..., None], axis=-2)
        hmid = jax.nn.gelu(jnp.einsum('bsc,ehc->bseh', xt, fc1_w) + fc1_b, approximate=False)
        hw = hmid * combine[..., None]
        out = jnp.einsum('bseh,ech->bsc', hw, fc2_w)
        out = out + jnp.einsum('bse,ec->bsc', combine, fc2_b)
        return out.reshape(b, h, w, c)

    def _gn(v, G=32, eps=1e-05):
        B_, H_, W_, C_ = v.shape
        g = v.reshape(B_, H_, W_, G, C_ // G)
        m = jnp.mean(g, axis=(1, 2, 4), keepdims=True)
        s = jnp.var(g, axis=(1, 2, 4), keepdims=True)
        return ((g - m) / jnp.sqrt(s + eps)).reshape(v.shape)

    def _ln_c(v, eps=1e-06):
        m = jnp.mean(v, axis=-1, keepdims=True)
        s = jnp.var(v, axis=-1, keepdims=True)
        return (v - m) / jnp.sqrt(s + eps)

    def _ln_t(v, eps=1e-05):
        m = jnp.mean(v, axis=-1, keepdims=True)
        s = jnp.var(v, axis=-1, keepdims=True)
        return (v - m) / jnp.sqrt(s + eps)

    def _to_tokens(v):
        B_, H_, W_, C_ = v.shape
        return v.reshape(B_, H_ * W_, C_)

    def _from_tokens(t, like):
        return t.reshape(like.shape)
    x = x + _L0_conv_ref(_gn(x), L0_conv_registers, L0_conv_qkv_w, L0_conv_qkv_b, L0_conv_out_w, L0_conv_out_b)
    x = x + _L1_conv_ref(_gn(x), L1_conv_router_w, L1_conv_router_b, L1_conv_fc1_w, L1_conv_fc1_b, L1_conv_fc2_w, L1_conv_fc2_b)
    return x

_drawn_inputs = setup_inputs


def setup_inputs(seed=0):
    import zlib

    import numpy as np

    out = dict(_drawn_inputs(seed))
    spreads = {'L1_conv_router_b': (0.0, 0.1)}
    factors = {'L0_conv_qkv_b': 2.865, 'L1_conv_fc1_b': 8.0, 'L1_conv_fc2_b': 8.0}
    for name, (base, spread) in spreads.items():
        noise = np.random.default_rng([zlib.crc32(name.encode()), seed]).standard_normal(out[name].shape)
        drawn = base * np.exp(spread * noise) if base else spread * noise
        out[name] = jnp.asarray(drawn.astype(out[name].dtype))
    for name, factor in factors.items():
        out[name] = (out[name] * factor).astype(out[name].dtype)
    return out
```

```python
import concourse.bass as bass
import concourse.mybir as mybir
from contextlib import ExitStack

F32, F16, BF16, U16 = mybir.dt.float32, mybir.dt.float16, mybir.dt.bfloat16, mybir.dt.uint16
ALU, ACT = mybir.AluOpType, mybir.ActivationFunctionType
AX = mybir.AxisListType.X

IMAGES, H, W, C = 2, 48, 48, 384
N = H * W
P = 128
KC = C // P
HEADS, DH = 4, 32
REGS = 16
WIN = 7
TR, TC = 8, 16
STRIPS, TPS = H // TR, W // TC
TILES = STRIPS * TPS
SN = TPS * P
RR, RC = TR + WIN - 1, TC + WIN - 1
RK = RR * RC
KEYS = RK + REGS
ROWS = (5, 5, 4)
LEN = (5 * RC, 5 * RC, 4 * RC + REGS)
AT = (0, 5 * RC, 10 * RC)
GROUPS, EPS = 32, 1e-5
WS = 16.0
SCORE = DH ** -0.5 / WS ** 2
EXPERTS, HID = 4, 96
LAST0 = H - TR - 3
PADROWS = LAST0 + RR - H
KPAD = PADROWS * W
STAGES = IMAGES * KC
GCH = 768
GN_STEPS = KC * (N // GCH)


def build(nc, x, wqkv, wo, fc1, fc2, rw, regs, qkb, bv, ob, fb1, fb2, rb, masks, gmat, ident, ident16, tri, out):
    ctx = ExitStack()
    with ctx:
        sb = lambda name, shape, dt=F32: ctx.enter_context(nc.sbuf_tensor(name, shape, dt))
        sem = lambda name: ctx.enter_context(nc.semaphore(name))

        X = sb("X", [P, IMAGES * KC * N])
        XH = sb("XH", [P, IMAGES * 2 * KC * N], F16)
        QS = sb("QS", [P, HEADS * N], F16)
        KS = sb("KS", [P, HEADS * N + KPAD], F16)
        KRS = sb("KRS", [P, HEADS, KC, REGS], F16)
        WQ = sb("WQ", [P, 2, KC, 3 * C], F16)
        WO = sb("WO", [P, 2, KC, C], F16)
        OS = sb("OS", [P, 2 * N], F16)
        PT = sb("PT", [P, 2, HEADS, C])
        PR = sb("PR", [P, 2, KEYS])
        VR = sb("VR", [P, 2, 3, P])
        MK = sb("MK", [P, 2, TPS, KEYS], U16)
        O32 = sb("O32", [P, 2, P])
        RX = sb("RX", [P, 2, P])
        RB = sb("RB", [P, 2, P])
        ID = sb("ID", [P, P])
        QT = sb("QT", [P, 2, 2, SN], F16)
        KT = sb("KT", [P, 2, 2, SN], F16)
        VT = sb("VT", [P, 2, TPS, P])
        BV = sb("BV", [P, C])
        KR = sb("KR", [P, 2, KC, REGS], F16)
        RG = sb("RG", [P, 2, KC, REGS], F16)
        SM = sb("SM", [P, 116])
        ps = ctx.enter_context(nc.psum_tensor("ps", [P, 8, 512], F32))

        cols, at = {}, 0
        for name, n in (("qkb", 6), ("qkb16", 6), ("ob", 3), ("fb1", 3), ("rb", 4), ("mv", 6), ("sq", 3),
                        ("gs", 6), ("var", 3), ("sd", 3), ("rstd", 3), ("nb", 3), ("negm", 8), ("rs", 8), ("ri", 8), ("credit", 43)):
            cols[name] = SM[:, at:at + n]
            at += n
        assert at <= 116
        negm = cols["negm"].rearrange("p (t h) -> p t h", t=2)
        rs = cols["rs"].rearrange("p (t h) -> p t h", t=2)
        ri = cols["ri"].rearrange("p (t h) -> p t h", t=2)
        mv = cols["mv"].rearrange("p (c s) -> p c s", s=2)
        gs = cols["gs"].rearrange("p (c s) -> p c s", s=2)

        wraw = QS[:, 0:2 * 3 * KC * C].bitcast(F32)
        oraw = KS[:, 0:2 * KC * C].bitcast(F32)
        rraw = KS[:, 2 * KC * C:2 * KC * C + 2 * KC * REGS].bitcast(F32)
        vreg_sb = KS[:, 4096:4096 + 2 * C].bitcast(F32)
        ptf = PT[:, :, :, :].rearrange("p a h n -> p (a h n)")
        gtmp = ptf[:, 0:2 * GCH].rearrange("p (t n) -> p t n", t=2)
        G = ptf[:, 2 * GCH:2 * GCH + KC * C].rearrange("p (k n) -> p k n", k=KC)
        st6 = O32[:, :, :].rearrange("p t n -> p (t n)")[:, 0:KC * STRIPS * 6].rearrange("p (c s e) -> p c s e", c=KC, e=6)
        fcw = WQ[:, :, :, :].rearrange("p s k n -> p (s k n)")
        W1 = fcw[:, 0:2 * KC * C].rearrange("p (s k n) -> p s k n", s=2, k=KC)
        W2 = fcw[:, 2 * KC * C:4 * KC * C].rearrange("p (s k n) -> p s k n", s=2, k=KC)
        RWs = fcw[:, 4 * KC * C:4 * KC * C + 2 * KC * EXPERTS].rearrange("p (s k n) -> p s k n", s=2, k=KC)
        f1raw = QS[:, 0:2 * KC * C].bitcast(F32)
        f2raw = QS[:, 2 * KC * C:4 * KC * C].bitcast(F32)
        rwraw = QS[:, 4 * KC * C:4 * KC * C + 2 * KC * EXPERTS].bitcast(F32)
        b2raw = QS[:, 4 * KC * C + 64:4 * KC * C + 64 + 2 * C].bitcast(F32)
        G2 = QS[:, 6 * KC * C:8 * KC * C].bitcast(F32).rearrange("p (k n) -> p k n", k=KC)
        B2 = OS[:, 0:C]
        HW = ptf.bitcast(F16)[:, 0:12 * SN].rearrange("p (a s k n) -> p a s k n", a=2, s=2, k=KC)
        k32 = KS[:, 0:4 * 2304].bitcast(F32)
        GE = k32[:, 0:2 * SN].rearrange("p (t n) -> p t n", t=2)
        HF = k32[:, 2 * SN:4 * SN].rearrange("p (t n) -> p t n", t=2)
        CX = k32[:, 4 * SN:4 * SN + 2 * C].rearrange("p (t n) -> p t n", t=2)
        r32 = k32[:, 6 * SN:]
        LG = r32[:, 0:72].rearrange("p (t e) -> p t e", e=EXPERTS)
        EX = r32[:, 72:144].rearrange("p (t e) -> p t e", e=EXPERTS)
        SE = r32[:, 144:216].rearrange("p (t e) -> p t e", e=EXPERTS)
        CB = r32[:, 216:288].rearrange("p (t e) -> p t e", e=EXPERTS)
        RK_ = r32[:, 288:360].rearrange("p (t e) -> p t e", e=EXPERTS)
        M1 = r32[:, 360:378]
        ZS = r32[:, 378:396]
        S2 = r32[:, 396:414]
        TRI = r32[:, 416:432].rearrange("p (i j) -> p i j", j=EXPERTS)
        GT = r32[:, 432:720].rearrange("p (t i j) -> p t i j", i=EXPERTS, j=EXPERTS)
        EQ = r32[:, 720:1008].rearrange("p (t i j) -> p t i j", i=EXPERTS, j=EXPERTS)
        c16 = OS[:, C:]
        CH = c16[:, 0:72].rearrange("p (t e) -> p t e", e=EXPERTS)
        CL = c16[:, 72:144].rearrange("p (t e) -> p t e", e=EXPERTS)
        CS = c16[:, 144:336].rearrange("p (t n) -> p t n", t=2)
        CT = c16[:, 336:336 + 2 * SN].rearrange("p (t n) -> p t n", t=2)
        ID16 = c16[:, 336 + 2 * SN:336 + 2 * SN + P]

        vscr = nc.dram_tensor("vscr", [N + PADROWS * W, P], F32, kind="Internal").ap()
        vrscr = nc.dram_tensor("vrscr", [REGS, C], F32, kind="Internal").ap()
        qkscr = nc.dram_tensor("qkscr", [2, 2, P, N], F16, kind="Internal").ap()
        krscr = nc.dram_tensor("krscr", [2, P, KC * REGS], F16, kind="Internal").ap()
        v_rows = vscr.rearrange("(r c) d -> r c d", c=W)
        v_tiles = vscr[0:N, :].rearrange("(a r b c) d -> a b r c d", r=TR, b=TPS, c=TC)

        xs = lambda img, c, n0, n: X[:, bass.ds(img * (KC * N) + c * N + n0, n)]
        xh = lambda img, s, c, n0, n: XH[:, bass.ds(img * (2 * KC * N) + (s * KC + c) * N + n0, n)]
        S_BANK = lambda h: ps[:, h, :]
        T_BANK = lambda i: ps[:, 4 + i, :]
        O_BANK = lambda i: ps[:, 6 + i, :]

        names = """w_in wo_in r_in c_in b_in id_in whi wlo wohi wolo rhi rlo b16 kr_mm kr_hi kr_lo vr_mm vr_sb vr_out
            x_in0 x_in1 chain gn_st gn_mm gn_var gn_sd gn_par gn_hi gn_t gn_lo
            q_mm k_mm v_mm q_hi k_hi q_lo k_lo v_sb q_in k_in kr_out krs_in vreg_in m_inner m_first m_next m_last pv norm ohi osplit rinv rx rbs op_mm op_done
            f_in fhi flo b2_in b2z b2s tri_in id16_in lg_mm ex_in ex_out comb csz cx_cs cb_mm ct_sb kpad vpad c2_in
            h_mm ge hf hh hl y_mm y_done y_out""".split()
        s = {n: sem(n) for n in names}
        q_out, k_out, v_out, v_in = ([sem(f"{n}{i}") for i in (0, 1)] for n in ("q_out", "k_out", "v_out", "v_in"))
        s_mm, ttr, exd, trd, evd = ([sem(f"{n}{h}") for h in range(HEADS)] for n in ("s_mm", "ttr", "exd", "trd", "evd"))
        CREDIT = 2
        credited = [s[n] for n in ("q_lo", "k_lo", "v_sb", "pv", "norm", "osplit", "op_done", "cb_mm", "ge", "hf", "hl",
                                   "y_done", "q_in", "k_in", "ct_sb")] + [ttr[3]] + q_out + k_out + v_out + v_in + s_mm + exd + trd + evd
        gone = lambda n: n + 1
        done = lambda n: n + 1 + CREDIT
        start = lambda n: n + CREDIT
        Y_CREDIT = 2 * KC

        def counted(eng, sem, count, least=1):
            count = eng.to_reg(count)
            eng.wait_ge(sem, least)
            eng.wait_ge(sem, count)

        block = ctx.enter_context(nc.Block())

        def strip_walk(eng, st, body):
            t0, p0 = eng.snap(st * TILES), eng.snap(st * (TILES // 2))
            body(0, 0, t0, p0)
            with eng.Fori(0, 2) as m:
                t1, p1 = eng.snap(st * TILES + m * 6), eng.snap(st * (TILES // 2) + m * 3)
                body(1, m, t1, p1)
                body(2, m, t1, p1)
            t2, p2 = eng.snap(st * TILES), eng.snap(st * (TILES // 2))
            body(5, 0, t2, p2)

        def x_strip(img, a):
            base = X[:, :].rearrange("p (i k n) -> p i k n", i=IMAGES, k=KC)
            return base[:, bass.ds(img, 1), :, bass.ds(a * SN, SN)].rearrange("p i k n -> p (i k) n")

        def expert_walk(eng, img, hidden, result):
            def both(i, m, prior):
                n0 = eng.snap(img * STRIPS + m * 2)
                hidden(i, n0 + i, m * 2 + i)
                if prior and result:
                    result(i - 1, n0 + (i - 1), m * 2 + (i - 1))
            both(0, 0, False)
            with eng.Fori(0, 2) as m:
                both(1, m, True)
                both(2, m, True)
            both(5, 0, True)
            if result:
                result(5, eng.snap(img * STRIPS + 5), 5)

        ct_bank = ps[0:96, 5, 0:SN // 2].bitcast(F16)
        def flat(t, part):
            return t[:, part, :, :].rearrange("p k n -> p (k n)")

        def region_view(ap):
            return bass.AP(ap.tensor, ap.offset, [list(ap.ap[0]), [W, RR], [1, RC]])

        raster = lambda ap: ap.rearrange("p (b r c) -> p r b c", r=TR, b=TPS)

        @block.sync
        def _(sp):
            for img in range(IMAGES):
                for c in range(KC):
                    sp.dma_start(xs(img, c, 0, N), x[img, :, c, :]).then_inc(s[f"x_in{img}"], 16)
            sp.wait_ge(s["kpad"], 1)
            zeros = KS[:, HEADS * N:].bitcast(F32)
            half = KPAD // 2
            for i in (0, 1):
                sp.dma_start(vscr[N + half * i:N + half * (i + 1), :].rearrange("r d -> (r d)").rearrange("(p n) -> p n", p=P),
                             zeros).then_inc(s["vpad"], 16)
            sp.wait_ge(s["vpad"], 32)
            sp.wait_ge(s["vr_sb"], 1)
            sp.dma_start(vrscr, vreg_sb[0:REGS, :]).then_inc(s["vr_out"], 16)
            sp.wait_ge(s["vr_out"], 16)
            sp.wait_ge(s["kr_lo"], 1)
            sp.dma_start(krscr.rearrange("s p n -> p s n"), KR[:, :, :, :].rearrange("p s k r -> p s (k r)")).then_inc(s["kr_out"], 16)
            sp.wait_ge(s["kr_out"], 16)
            for j, part in enumerate((0, 1, 0)):
                sp.dma_start(KRS[DH * j:DH * (j + 1), :, :, :].rearrange("d h k r -> d h (k r)"),
                             krscr[part].rearrange("(h d) n -> d h n", d=DH)).then_inc(s["krs_in"], 16)
            sp.dma_start(MK[:, 0, :, :], masks[TPS:2 * TPS].rearrange("b p n -> p b n")).then_inc(s["m_inner"], 16)
            with sp.Fori(0, IMAGES) as img:
                with sp.Fori(0, KC) as g:
                    st = sp.snap(img * KC + g)
                    sp.wait_ge(ttr[3], st * TILES + CREDIT)
                    sp.dma_start(MK[:, 1, :, :], masks[0:TPS].rearrange("b p n -> p b n")).then_inc(s["m_first"], 16)
                    sp.wait_ge(s["pv"], st * TILES + CREDIT)
                    for i in (0, 1):
                        sp.dma_start(VR[4 * RC:4 * RC + REGS, i, 2, :], vrscr[:, bass.ds(g * P, P)]).then_inc(s["vreg_in"], 16)
                        counted(sp, v_in[i], st * (TILES // 2 * 48) + CREDIT)
                    for h in range(HEADS):
                        sp.wait_ge(s_mm[h], st * TILES + CREDIT)

                    def pair(m):
                        use = sp.snap(st * (STRIPS // 2) + m)
                        sp.wait_ge(s["q_in"], use * 48 + CREDIT)
                        sp.wait_ge(s["k_in"], use * 48 + CREDIT)
                        for i in (0, 1):
                            n = sp.snap(st * STRIPS + m * 2 + i)
                            for q, (stage, name, full, moved) in enumerate(((QT, "q", q_out, s["q_lo"]), (KT, "k", k_out, s["k_lo"]))):
                                counted(sp, s[name + "_hi"], n + 1)
                                counted(sp, moved, done(n))
                                sp.dma_start(qkscr[q].rearrange("s p n -> p s n")[:, :, bass.ds(m * (2 * SN) + i * SN, SN)],
                                             stage[:, i, :, :]).then_inc(full[i], 16)
                            counted(sp, s["v_sb"], done(n))
                            for b in range(TPS):
                                sp.dma_start(v_tiles[bass.ds(m * 2 + i, 1), b].rearrange("a r c d -> (a r) c d"),
                                             VT[:, i, b, :]).then_inc(v_out[i], 16)
                        for q, (stack, full, name, parts) in enumerate(((QS, q_out, "q_in", (0, 0, 1)), (KS, k_out, "k_in", (0, 1, 0)))):
                            for i in (0, 1):
                                counted(sp, full[i], use * 16 + 16 + CREDIT, 16 + CREDIT)
                            for j, part in enumerate(parts):
                                sp.dma_start(stack[DH * j:DH * (j + 1), 0:HEADS * N].rearrange("d (h n) -> d h n", h=HEADS)[
                                                 :, :, bass.ds(m * (2 * SN), 2 * SN)],
                                             qkscr[q, part].rearrange("(h d) n -> d h n", d=DH)[:, :, bass.ds(m * (2 * SN), 2 * SN)]
                                             ).then_inc(s[name], 16)
                        for i in (0, 1):
                            counted(sp, v_out[i], use * 48 + 48 + CREDIT, 48 + CREDIT)

                    def region(t, row0, tile0):
                        sp.wait_ge(s["pv"], gone(tile0 + t))
                        x0 = 13 * (t % TPS)
                        for c in range(3):
                            sp.dma_start(VR[0:ROWS[c] * RC, t % 2, c, :],
                                         v_rows[bass.ds(row0 + 5 * c, ROWS[c]), x0:x0 + RC, :]).then_inc(v_in[t % 2], 16)

                    def regions(i, m, tile0, pair0):
                        row0 = 0 if i == 0 else LAST0 if i == 5 else sp.snap(m * (2 * TR) + (i * TR - 3))
                        for b in range(TPS):
                            t = TPS * i + b
                            if t >= 2:
                                region(t, row0, tile0)
                        if i == 1:
                            sp.wait_ge(ttr[3], done(tile0 + TPS))
                            sp.dma_start(MK[:, 1, 0, :], masks[bass.ds(m * TPS + TPS, 1)].rearrange("a p n -> (a p) n")).then_inc(s["m_next"], 16)
                        if i == 0:
                            sp.wait_ge(ttr[3], done(tile0 + (TPS - 1)))
                            sp.dma_start(MK[:, 1, 1:TPS, :], masks[2 * TPS + 1:3 * TPS].rearrange("b p n -> p b n")).then_inc(s["m_last"], 16)

                    with sp.Fori(0, STRIPS // 2 - 1) as m:
                        pair(m)
                    for t in (0, 1):
                        region(t, 0, sp.snap(st * TILES))
                    pair(STRIPS // 2 - 1)
                    strip_walk(sp, st, regions)
            sp.wait_ge(s_mm[3], STAGES * TILES + CREDIT)
            sp.wait_ge(s["op_done"], STAGES * STRIPS + CREDIT)
            for src, dst in ((fc1, f1raw), (fc2, f2raw), (rw, rwraw)):
                sp.dma_start(dst, src).then_inc(s["f_in"], 16)
            for j in range(3):
                sp.dma_start(b2raw[DH * j:DH * j + EXPERTS, :], fb2).then_inc(s["b2_in"], 16)
            sp.dma_start(TRI.rearrange("p i j -> p (i j)"), tri).then_inc(s["tri_in"], 16)
            sp.dma_start(ID16, ident16).then_inc(s["id16_in"], 16)
            sp.dma_start(G2, gmat).then_inc(s["c2_in"], 16)
            with sp.Fori(0, IMAGES) as img:
                with sp.Fori(0, STRIPS) as a:
                    n = sp.snap(img * STRIPS + a)
                    sp.wait_ge(s["y_done"], n * KC + KC + CREDIT)
                    sp.dma_start(out[bass.ds(img, 1), :, :, bass.ds(a * SN, SN)].rearrange("i p k n -> (i p) k n"),
                                 x_strip(img, a)).then_inc(s["y_out"], 16)
            sp.wait_ge(s["y_out"], 16 * IMAGES * STRIPS)

        @block.gpsimd
        def _(pool):
            nc.gpsimd.memset(KS[:, HEADS * N:], 0.0).then_inc(s["kpad"], 1)
            for src, dst, name in ((wqkv, wraw, "w_in"), (regs, rraw, "r_in"), (gmat, G, "c_in"), (wo, oraw, "wo_in"),
                                   (ident, ID[:, :], "id_in"), (bv.partition_broadcast(P), BV[:, :], "b_in"),
                                   (qkb, cols["qkb"], "b_in"), (ob, cols["ob"], "b_in"), (fb1, cols["fb1"], "b_in"),
                                   (rb.partition_broadcast(P), cols["rb"], "b_in")):
                pool.dma_start(dst, src).then_inc(s[name], 16)

            def low_halves(img, n):
                for i in range(GN_STEPS):
                    c, n0 = divmod(i * GCH, N)
                    pool.wait_ge(s["gn_t"], n * GN_STEPS + i + 1)
                    pool.wait_ge(s["gn_hi"], n * GN_STEPS + i + 1)
                    nc.gpsimd.tensor_tensor(xh(img, 1, c, n0, GCH), gtmp[:, i % 2, :], xh(img, 0, c, n0, GCH),
                                            ALU.subtract).then_inc(s["gn_lo"], 1)

            for img in range(IMAGES):
                low_halves(img, img)
            with pool.Fori(0, STAGES) as st:
                def split(t, n0, tile0):
                    counted(pool, s["norm"], done(tile0 + t))
                    hi, lo = OS[:, bass.ds(n0, P)], OS[:, bass.ds(n0 + N, P)]
                    nc.gpsimd.tensor_copy(hi, O32[:, t % 2, :]).then_inc(s["ohi"], 1)
                    pool.wait_ge(s["ohi"], tile0 + t + 1)
                    nc.gpsimd.tensor_tensor(lo, O32[:, t % 2, :], hi, ALU.subtract).then_inc(s["osplit"], 1)

                def step(i, m, tile0, pair0):
                    for b in range(TPS):
                        t = 3 * i + b
                        counted(pool, s["pv"], gone(tile0 + t))
                        counted(pool, s["rinv"], tile0 + t + 1)
                        nc.gpsimd.tensor_copy(RX[:, t % 2, :].rearrange("p (h d) -> p h d", h=HEADS),
                                              ri[:, t % 2, :].unsqueeze(2).broadcast_to([P, HEADS, DH])).then_inc(s["rx"], 1)
                        if t >= 2:
                            split(t - 2, pool.snap(m * (2 * SN) + (t - 2) * P), tile0)
                strip_walk(pool, st, step)
                for t in (TILES - 2, TILES - 1):
                    split(t, pool.snap(st * 0 + t * P), pool.snap(st * TILES))
            pool.wait_ge(s["op_done"], STAGES * STRIPS + CREDIT)
            nc.gpsimd.memset(CS, 0.0).then_inc(s["csz"], 1)
            pool.wait_ge(s["csz"], 1)
            with pool.Fori(0, IMAGES) as img:
                low_halves(img, pool.snap(img + IMAGES))
                counted(pool, s["comb"], img + 1)
                with pool.Fori(0, STRIPS // 2) as m:
                    for i in range(2 * TPS):
                        tile = pool.snap(img * TILES + m * (2 * TPS) + i)
                        e0 = pool.snap(m * (2 * TPS * EXPERTS) + i * EXPERTS)
                        pool.wait_ge(s["cb_mm"], gone(tile))
                        one = lambda ap: ap.rearrange("p t e -> p (t e)")[:, bass.ds(e0, EXPERTS)]
                        nc.gpsimd.tensor_copy(CX[:, i % 2, :].rearrange("p (e h) -> p e h", e=EXPERTS),
                                              one(CB).unsqueeze(2).broadcast_to([P, EXPERTS, HID]))
                        for j, part in enumerate((CH, CL, CH)):
                            last = nc.gpsimd.tensor_copy(CS[:, i % 2, DH * j:DH * j + EXPERTS], one(part))
                        last.then_inc(s["cx_cs"], 1)
                        if i % TPS == TPS - 1:
                            for k in range(KC):
                                unit = pool.snap(img * (STRIPS * KC) + m * (2 * KC) + (i // TPS * KC + k))
                                pool.wait_ge(s["hf"], done(unit))
                                pool.wait_ge(s["hh"], unit + 1)
                                nc.gpsimd.tensor_tensor(HW[:, i // TPS, 1, k, :], HF[:, (i // TPS * 3 + k) % 2, :],
                                                        HW[:, i // TPS, 0, k, :], ALU.subtract).then_inc(s["hl"], 1)

        @block.vector
        def _(dve):
            V = nc.vector
            for i, x_ in enumerate(credited):
                V.memset(cols["credit"][:, i:i + 1], 0.0).then_inc(x_, CREDIT)
            V.memset(cols["credit"][:, 42:43], 0.0).then_inc(s["y_mm"], Y_CREDIT)

            def chain(base):
                k = [0]

                def link(ins):
                    k[0] += 1
                    ins.then_inc(s["chain"], 1)
                    counted(dve, s["chain"], base + k[0])
                return link, k

            dve.wait_ge(s["w_in"], 16)
            dve.wait_ge(s["whi"], 1)
            V.scalar_tensor_tensor(out=flat(WQ, 1), in0=wraw, scalar=WS, in1=flat(WQ, 0), op0=ALU.mult,
                                   op1=ALU.subtract).then_inc(s["wlo"], 1)
            dve.wait_ge(s["b_in"], 16 * 5)
            V.tensor_scalar(cols["qkb16"], cols["qkb"], WS, None, ALU.mult).then_inc(s["b16"], 1)
            dve.wait_ge(s["r_in"], 16)
            dve.wait_ge(s["rhi"], 1)
            V.tensor_tensor(flat(RG, 1), rraw, flat(RG, 0), ALU.subtract).then_inc(s["rlo"], 1)
            dve.wait_ge(s["wo_in"], 16)
            dve.wait_ge(s["wohi"], 1)
            V.scalar_tensor_tensor(out=flat(WO, 1), in0=oraw, scalar=WS, in1=flat(WO, 0), op0=ALU.mult,
                                   op1=ALU.subtract).then_inc(s["wolo"], 1)
            dve.wait_ge(s["kr_hi"], 1)
            dve.wait_ge(s["b16"], 1)
            for g in range(KC):
                last = V.scalar_tensor_tensor(out=KR[:, 1, g, :], in0=ps[:, 0, REGS * g:REGS * (g + 1)],
                                              scalar=cols["qkb16"][:, KC + g:KC + g + 1], in1=KR[:, 0, g, :],
                                              op0=ALU.add, op1=ALU.subtract)
            last.then_inc(s["kr_lo"], 1)
            dve.wait_ge(s["vr_mm"], 1)
            V.scalar_tensor_tensor(out=vreg_sb[0:REGS, :], in0=ps[0:REGS, 1, 0:C], scalar=1 / WS, in1=BV[0:REGS, :],
                                   op0=ALU.mult, op1=ALU.add).then_inc(s["vr_sb"], 1)

            def group_norm(img, n, link):
                for c in range(KC):
                    for j in range(STRIPS):
                        last = V.bn_stats(st6[:, c, j, :], xs(img, c, j * SN, SN))
                link(last)
                for c in range(KC):
                    last = V.bn_aggr(mv[:, c, :], st6[:, c, :, :].rearrange("p s e -> p (s e)"))
                link(last)
                link(V.tensor_tensor(cols["sq"], mv[:, :, 0], mv[:, :, 0], ALU.mult))
                V.tensor_tensor(mv[:, :, 1], mv[:, :, 1], cols["sq"], ALU.add).then_inc(s["gn_st"], 1)
                dve.wait_ge(s["gn_mm"], n + 1)
                link(V.tensor_copy(cols["gs"], ps[:, 7, 0:2 * KC]))
                link(V.tensor_tensor(cols["sq"], gs[:, :, 0], gs[:, :, 0], ALU.mult))
                V.scalar_tensor_tensor(out=cols["var"], in0=gs[:, :, 1], scalar=EPS, in1=cols["sq"],
                                       op0=ALU.add, op1=ALU.subtract).then_inc(s["gn_var"], 1)
                dve.wait_ge(s["gn_sd"], n + 1)
                link(V.reciprocal(cols["rstd"], cols["sd"]))
                V.scalar_tensor_tensor(out=cols["nb"], in0=gs[:, :, 0], scalar=-1.0, in1=cols["rstd"],
                                       op0=ALU.mult, op1=ALU.mult).then_inc(s["gn_par"], 1)
                dve.wait_ge(s["gn_par"], n + 1)
                for i in range(GN_STEPS):
                    c, n0 = divmod(i * GCH, N)
                    if not (isinstance(n, int) and n * GN_STEPS + i < 2):
                        dve.wait_ge(s["gn_lo"], n * GN_STEPS + max(i - 1, 0))
                    V.tensor_scalar(gtmp[:, i % 2, :], xs(img, c, n0, GCH), cols["rstd"][:, c:c + 1],
                                    cols["nb"][:, c:c + 1], ALU.mult, ALU.add).then_inc(s["gn_t"], 1)

            GN_LINKS = 6
            for img in range(IMAGES):
                link, k = chain(img * (GN_LINKS + 1))
                dve.wait_ge(s[f"x_in{img}"], 16 * KC)
                group_norm(img, img, link)
                dve.wait_ge(s["gn_hi"], GN_STEPS * (img + 1))
                dve.wait_ge(s["gn_t"], GN_STEPS * (img + 1))
                for c in range(KC):
                    last = V.tensor_scalar(xs(img, c, 0, N), xs(img, c, 0, N), cols["ob"][:, c:c + 1], None, ALU.add)
                link(last)
                assert k[0] == GN_LINKS + 1

            def maxima(t, tile0, mask, heads):
                p = t % 2
                for h in heads:
                    counted(dve, s_mm[h], done(tile0 + t))
                    V.tensor_tensor_reduce(out=S_BANK(h)[:, 0:KEYS], in0=S_BANK(h)[:, 0:KEYS], in1=mask.bitcast(BF16),
                                           scale=-SCORE, scalar=3e38, op0=ALU.add, op1=ALU.min,
                                           accum_out=negm[:, p, h:h + 1]).then_inc(ttr[h], 1)

            def keys_out(t, tile0, h):
                dve.wait_ge(trd[h], done(tile0 + t))
                V.tensor_copy(PT[:, t % 2, h, :], T_BANK(h % 2)[:, 0:C]).then_inc(evd[h], 1)

            def normalise(t, tile0):
                p = t % 2
                dve.wait_ge(s["rbs"], tile0 + t + 1)
                dve.wait_ge(s["osplit"], gone(tile0 + t))
                V.tensor_tensor(O32[:, p, :], O_BANK(p)[:, 0:P], RB[:, p, :], ALU.mult).then_inc(s["norm"], 1)

            with dve.Fori(0, IMAGES) as img:
                with dve.Fori(0, KC) as g:
                    st = dve.snap(img * KC + g)
                    with dve.Fori(0, STRIPS // 2) as m:
                        for i in (0, 1):
                            n = dve.snap(st * STRIPS + m * 2 + i)
                            use = dve.snap(st * (STRIPS // 2) + m)
                            dve.wait_ge(s["q_hi"], n + 1)
                            dve.wait_ge(q_out[i], use * 16 + CREDIT)
                            V.scalar_tensor_tensor(out=QT[:, i, 1, :], in0=ps[:, 3 * i, 0:SN],
                                                   scalar=cols["qkb16"][:, bass.ds(g, 1)], in1=QT[:, i, 0, :],
                                                   op0=ALU.add, op1=ALU.subtract).then_inc(s["q_lo"], 1)
                            dve.wait_ge(s["k_hi"], n + 1)
                            dve.wait_ge(k_out[i], use * 16 + CREDIT)
                            V.scalar_tensor_tensor(out=KT[:, i, 1, :], in0=ps[:, 3 * i + 1, 0:SN],
                                                   scalar=cols["qkb16"][:, bass.ds(g + KC, 1)], in1=KT[:, i, 0, :],
                                                   op0=ALU.add, op1=ALU.subtract).then_inc(s["k_lo"], 1)
                            dve.wait_ge(s["v_mm"], n + 1)
                            dve.wait_ge(v_out[i], use * 48 + CREDIT)
                            V.scalar_tensor_tensor(out=VT[:, i, :, :], in0=ps[:, 3 * i + 2, 0:SN].rearrange("p (b n) -> p b n", b=TPS),
                                                   scalar=1 / WS, in1=BV[:, bass.ds(g * P, P)].unsqueeze(1).broadcast_to([P, TPS, P]),
                                                   op0=ALU.mult, op1=ALU.add).then_inc(s["v_sb"], 1)
                    dve.wait_ge(s["m_inner"], 16)
                    dve.wait_ge(s["m_first"], st * 16 + 16)
                    maxima(0, dve.snap(st * TILES), MK[:, 1, 0, :], range(HEADS))

                    def step(i, m, tile0, pair0):
                        for b in range(TPS):
                            t = 3 * i + b
                            more = t < TILES - 1
                            a1, b1 = divmod(t + 1, TPS)
                            mask = MK[:, 0 if a1 in (1, 2) else 1, b1, :]
                            if a1 == 3:
                                dve.wait_ge(s["m_next"], st * 32 + m * 16 + 16)
                            elif t == TILES - TPS:
                                dve.wait_ge(s["m_last"], st * 16 + 16)
                            if more:
                                maxima(t + 1, tile0, mask, (0,))
                            keys_out(t, tile0, 1)
                            if t >= 2:
                                normalise(t - 2, tile0)
                            if more:
                                maxima(t + 1, tile0, mask, (1, 2))
                            keys_out(t, tile0, 3)
                            if more:
                                maxima(t + 1, tile0, mask, (3,))
                            dve.wait_ge(exd[3], done(tile0 + t))
                            V.reciprocal(ri[:, t % 2, :], rs[:, t % 2, :]).then_inc(s["rinv"], 1)
                    strip_walk(dve, st, step)
                    for t in (TILES - 2, TILES - 1):
                        normalise(t, dve.snap(st * TILES))
                    with dve.Fori(0, STRIPS // 2) as m:
                        for i in (0, 1):
                            n = dve.snap(st * STRIPS + m * 2 + i)
                            dve.wait_ge(s["op_mm"], n + 1)
                            for j in range(KC):
                                xj = xs(img, j, m * (2 * SN) + i * SN, SN)
                                last = V.scalar_tensor_tensor(out=xj, in0=ps[:, 3 * i + j, 0:SN], scalar=1 / WS, in1=xj,
                                                              op0=ALU.mult, op1=ALU.add)
                            last.then_inc(s["op_done"], 1)
            dve.wait_ge(s["op_done"], STAGES * STRIPS + CREDIT)
            dve.wait_ge(s["fhi"], 3)
            for raw, w, name in ((f1raw, W1, "flo"), (f2raw, W2, "flo"), (rwraw, RWs, "flo")):
                V.scalar_tensor_tensor(out=flat(w, 1), in0=raw, scalar=WS, in1=flat(w, 0), op0=ALU.mult,
                                       op1=ALU.subtract).then_inc(s[name], 1)
            dve.wait_ge(s["b2s"], 1)
            V.scalar_tensor_tensor(out=B2[64:68, :], in0=b2raw[64:68, :], scalar=WS, in1=B2[64:68, :], op0=ALU.mult,
                                   op1=ALU.subtract).then_inc(s["flo"], 1)
            dve.wait_ge(s["tri_in"], 16)
            BASE = IMAGES * (GN_LINKS + 1)
            LINKS = GN_LINKS + 13
            with dve.Fori(0, IMAGES) as img:
                link, k = chain(dve.snap(img * LINKS + BASE))
                group_norm(img, dve.snap(img + IMAGES), link)
                dve.wait_ge(s["lg_mm"], img * TILES + TILES)
                bc = lambda ap: ap.unsqueeze(2).broadcast_to([P, TILES, EXPERTS])
                link(V.scalar_tensor_tensor(out=LG, in0=ps[:, 7, 0:TILES * EXPERTS].rearrange("p (t e) -> p t e", e=EXPERTS),
                                            scalar=1 / WS, in1=cols["rb"].unsqueeze(1).broadcast_to([P, TILES, EXPERTS]),
                                            op0=ALU.mult, op1=ALU.add))
                link(V.reduce_max(M1, LG, AX))
                V.tensor_tensor(EX, LG, bc(M1), ALU.subtract).then_inc(s["ex_in"], 1)
                pair = [P, TILES, EXPERTS, EXPERTS]
                lj, li = LG.unsqueeze(2).broadcast_to(pair), LG.unsqueeze(3).broadcast_to(pair)
                V.tensor_tensor(GT, lj, li, ALU.is_gt)
                link(V.tensor_tensor(EQ, lj, li, ALU.is_equal))
                link(V.tensor_tensor(EQ, EQ, TRI.unsqueeze(1).broadcast_to(pair), ALU.mult))
                link(V.tensor_tensor(GT, GT, EQ, ALU.add))
                link(V.reduce_sum(RK_, GT, AX))
                link(V.tensor_scalar(RK_, RK_, 1.5, None, ALU.is_lt))
                dve.wait_ge(s["ex_out"], img + 1)
                link(V.tensor_tensor(SE, EX, RK_, ALU.mult))
                V.reduce_sum(ZS, EX, AX)
                link(V.reduce_sum(S2, SE, AX))
                link(V.scalar_tensor_tensor(out=S2, in0=ZS, scalar=1e-8, in1=S2, op0=ALU.mult, op1=ALU.add))
                link(V.reciprocal(S2, S2))
                link(V.tensor_tensor(CB, SE, bc(S2), ALU.mult))
                link(V.tensor_copy(CH, CB))
                V.tensor_tensor(CL, CB, CH, ALU.subtract).then_inc(s["comb"], 1)
                assert k[0] == LINKS

                def weigh(i, n, a):
                    dve.wait_ge(s["cb_mm"], n * TPS + TPS + CREDIT)
                    for k_ in range(KC):
                        u, unit = (3 * i + k_) % 2, n * KC + k_
                        dve.wait_ge(s["ge"], done(unit))
                        dve.wait_ge(s["hl"], gone(unit))
                        V.tensor_tensor(HF[:, u, :], ps[:, 2 + k_, 0:SN], GE[:, u, :], ALU.mult).then_inc(s["hf"], 1)

                def result(i, n, a):
                    for j in range(KC):
                        xj = xs(img, j, a * SN, SN)
                        dve.wait_ge(s["y_mm"], n * KC + j + 1 + Y_CREDIT)
                        V.scalar_tensor_tensor(out=xj, in0=ps[:, 6 + (3 * i + j) % 2, 0:SN], scalar=1 / WS, in1=xj,
                                               op0=ALU.mult, op1=ALU.add).then_inc(s["y_done"], 1)

                expert_walk(dve, img, weigh, result)

        @block.scalar
        def _(act):
            A = nc.scalar.activation
            for sem_in, raw, w, scale, name in (("w_in", wraw, WQ, WS, "whi"), ("r_in", rraw, RG, 1.0, "rhi"),
                                                ("wo_in", oraw, WO, WS, "wohi")):
                act.wait_ge(s[sem_in], 16)
                A(flat(w, 0), raw, ACT.Copy, scale=scale).then_inc(s[name], 1)
            act.wait_ge(s["kr_mm"], 1)
            act.wait_ge(s["b16"], 1)
            for g in range(KC):
                last = A(KR[:, 0, g, :], ps[:, 0, REGS * g:REGS * (g + 1)], ACT.Identity,
                         bias=cols["qkb16"][:, KC + g:KC + g + 1])
            last.then_inc(s["kr_hi"], 1)

            def group_norm(img, n):
                act.wait_ge(s["gn_var"], n + 1)
                A(cols["sd"], cols["var"], ACT.Sqrt).then_inc(s["gn_sd"], 1)
                act.wait_ge(s["gn_par"], n + 1)
                for i in range(GN_STEPS):
                    c, n0 = divmod(i * GCH, N)
                    A(xh(img, 0, c, n0, GCH), xs(img, c, n0, GCH), ACT.Identity, bias=cols["nb"][:, c:c + 1],
                      scale=cols["rstd"][:, c:c + 1]).then_inc(s["gn_hi"], 1)

            for img in range(IMAGES):
                group_norm(img, img)

            def keys_out(t, tile0, h):
                act.wait_ge(trd[h], done(tile0 + t))
                nc.scalar.copy(PT[:, t % 2, h, :], T_BANK(h % 2)[:, 0:C]).then_inc(evd[h], 1)

            def rb_out(t, tile0):
                act.wait_ge(s["pv"], done(tile0 + t))
                nc.scalar.copy(RB[:, t % 2, :], O_BANK(t % 2)[:, P:2 * P]).then_inc(s["rbs"], 1)

            def exps(t, tile0, heads):
                p = t % 2
                for h in heads:
                    act.wait_ge(ttr[h], tile0 + t + 1 + (CREDIT if h == 3 else 0))
                    act.wait_ge(trd[(h + 2) % 4], start(tile0 + t + (1 if h >= 2 else 0)))
                    A(PR[:, h % 2, :], S_BANK(h)[:, 0:KEYS], ACT.Exp, bias=negm[:, p, h:h + 1], scale=-1.0,
                      accum_out=rs[:, p, h:h + 1]).then_inc(exd[h], 1)

            with act.Fori(0, IMAGES) as img:
                with act.Fori(0, KC) as g:
                    st = act.snap(img * KC + g)
                    with act.Fori(0, STRIPS // 2) as m:
                        for i in (0, 1):
                            n = act.snap(st * STRIPS + m * 2 + i)
                            use = act.snap(st * (STRIPS // 2) + m)
                            counted(act, s["q_mm"], n + 1)
                            act.wait_ge(q_out[i], use * 16 + CREDIT)
                            A(QT[:, i, 0, :], ps[:, 3 * i, 0:SN], ACT.Identity, bias=cols["qkb16"][:, bass.ds(g, 1)]
                              ).then_inc(s["q_hi"], 1)
                            counted(act, s["k_mm"], n + 1)
                            act.wait_ge(k_out[i], use * 16 + CREDIT)
                            A(KT[:, i, 0, :], ps[:, 3 * i + 1, 0:SN], ACT.Identity,
                              bias=cols["qkb16"][:, bass.ds(g + KC, 1)]).then_inc(s["k_hi"], 1)

                    def step(i, m, tile0, pair0):
                        for b in range(TPS):
                            t = 3 * i + b
                            exps(t, tile0, (1,))
                            if t >= 2:
                                rb_out(t - 2, tile0)
                            keys_out(t, tile0, 0)
                            exps(t, tile0, (2, 3))
                            keys_out(t, tile0, 2)
                            if t < TILES - 1:
                                exps(t + 1, tile0, (0,))
                    exps(0, act.snap(st * TILES), (0,))
                    strip_walk(act, st, step)
                    for t in (TILES - 2, TILES - 1):
                        rb_out(t, act.snap(st * TILES))
            act.wait_ge(s["f_in"], 48)
            for raw, w in ((f1raw, W1), (f2raw, W2), (rwraw, RWs)):
                A(flat(w, 0), raw, ACT.Copy, scale=WS).then_inc(s["fhi"], 1)
            A(B2, oraw[:, 0:C], ACT.Copy, scale=0.0).then_inc(s["b2z"], 1)
            act.wait_ge(s["b2z"], 1)
            act.wait_ge(s["b2_in"], 48)
            for j in range(3):
                last = A(B2[DH * j:DH * j + EXPERTS, :], b2raw[DH * j:DH * j + EXPERTS, :], ACT.Copy, scale=WS)
            last.then_inc(s["b2s"], 1)
            with act.Fori(0, IMAGES) as img:
                group_norm(img, act.snap(img + IMAGES))
                act.wait_ge(s["ex_in"], img + 1)
                A(EX, EX, ACT.Exp).then_inc(s["ex_out"], 1)

                def hidden(i, n, a):
                    for k_ in range(KC):
                        u, unit = (3 * i + k_) % 2, n * KC + k_
                        act.wait_ge(s["h_mm"], unit + 1)
                        act.wait_ge(s["hf"], gone(unit))
                        A(GE[:, u, :], ps[:, u, 0:SN], ACT.Gelu, bias=cols["fb1"][:, k_:k_ + 1], scale=1 / WS
                          ).then_inc(s["ge"], 1)
                    act.wait_ge(s["y_mm"], n * KC + KC)
                    act.wait_ge(s["cb_mm"], n * TPS + TPS + CREDIT)
                    nc.scalar.copy(CT[0:96, i % 2, :], ct_bank).then_inc(s["ct_sb"], 1)
                    for k_ in range(KC):
                        u, unit = (3 * i + k_) % 2, n * KC + k_
                        act.wait_ge(s["hf"], done(unit))
                        nc.scalar.copy(HW[:, i % 2, 0, k_, :], HF[:, u, :]).then_inc(s["hh"], 1)

                expert_walk(act, img, hidden, None)

        @block.tensor
        def _(pe):
            mm = nc.tensor.matmul

            def split_product(bank, lhsT, rhs, steps=KC, finish=True):
                for k in range(steps):
                    for n, (a, b) in enumerate(((0, 0), (0, 1), (1, 0))):
                        last = mm(bank, lhsT(a, k), rhs(b, k), start=(k == 0 and n == 0),
                                  stop=(finish and k == steps - 1 and n == 2))
                return last

            pe.wait_ge(s["wlo"], 1)
            pe.wait_ge(s["rlo"], 1)
            for g in range(KC):
                last = split_product(ps[:, 0, REGS * g:REGS * (g + 1)], lambda a, k: WQ[:, a, k, C + g * P:C + (g + 1) * P],
                                     lambda b, k: RG[:, b, k, :])
            last.then_inc(s["kr_mm"], 1)
            split_product(ps[0:REGS, 1, 0:C], lambda a, k: RG[:, a, k, :], lambda b, k: WQ[:, b, k, 2 * C:3 * C]
                          ).then_inc(s["vr_mm"], 1)

            def group_means(n, G):
                pe.wait_ge(s["gn_st"], n + 1)
                for j in range(KC):
                    for k in range(KC):
                        last = mm(ps[:, 7, 2 * j:2 * j + 2], G[:, k, j * P:(j + 1) * P], mv[:, k, :], start=(k == 0), stop=(k == KC - 1))
                last.then_inc(s["gn_mm"], 1)

            pe.wait_ge(s["c_in"], 16)
            for img in range(IMAGES):
                group_means(img, G)
            pe.wait_ge(s["kr_lo"], 1)
            pe.wait_ge(s["vr_sb"], 1)
            pe.wait_ge(s["wolo"], 1)
            pe.wait_ge(s["id_in"], 16)

            def scores(t, m, tile0, g, h, row0, b):
                pe.wait_ge(exd[h], start(tile0 + t))
                q = QS[0:96, bass.ds(m * (2 * SN) + (h * N + t * P), P)]
                k0 = h * N + 13 * b
                span = (RR - 1) * W + RC
                if isinstance(row0, int):
                    base = KS[0:96, k0 + row0 * W:k0 + row0 * W + span]
                else:
                    base = KS[0:96, bass.ds(row0 * W + k0, span)]
                mm(S_BANK(h)[:, 0:RK], q, region_view(base), start=True, stop=True)
                mm(S_BANK(h)[:, RK:KEYS], q, KRS[0:96, h, :, :].rearrange("p k r -> p (k r)")[:, bass.ds(g * REGS, REGS)], start=True, stop=True
                   ).then_inc(s_mm[h], 1)

            def transposes(t, tile0, h):
                pe.wait_ge(exd[h], done(tile0 + t))
                pe.wait_ge(evd[(h + 2) % 4], start(tile0 + t + (1 if h >= 2 else 0)))
                for c in range(3):
                    last = nc.tensor.transpose(T_BANK(h % 2)[0:LEN[c], c * P:(c + 1) * P], PR[:, h % 2, AT[c]:AT[c] + LEN[c]], ID[:, :])
                last.then_inc(trd[h], 1)

            def values(t, tile0, pair0, c):
                p = t % 2
                if c == 0:
                    values_ready(t, tile0, pair0)
                for h in range(HEADS):
                    mm(O_BANK(p)[DH * h:DH * (h + 1), 0:P], VR[0:LEN[c], p, c, DH * h:DH * (h + 1)],
                       PT[0:LEN[c], p, h, c * P:(c + 1) * P], start=(c == 0), stop=(c == 2))
                if c == 2:
                    pe.wait_ge(s["rx"], tile0 + t + 1)
                    nc.tensor.transpose(O_BANK(p)[:, P:2 * P], RX[:, p, :], ID[:, :]).then_inc(s["pv"], 1)

            def values_ready(t, tile0, pair0):
                p = t % 2
                for h in range(HEADS):
                    pe.wait_ge(evd[h], done(tile0 + t))
                pe.wait_ge(v_in[p], start((pair0 + t // 2 + 1) * 48))
                pe.wait_ge(s["norm"], gone(tile0 + t))

            with pe.Fori(0, IMAGES) as img:
                with pe.Fori(0, KC) as g:
                    st = pe.snap(img * KC + g)
                    counted(pe, s["gn_lo"], img * GN_STEPS + GN_STEPS)
                    counted(pe, s["op_done"], st * STRIPS + CREDIT)
                    with pe.Fori(0, STRIPS // 2) as m:
                        for i in (0, 1):
                            n = pe.snap(st * STRIPS + m * 2 + i)
                            x_ = lambda b, k: xh(img, b, k, m * (2 * SN) + i * SN, SN)
                            pe.wait_ge(s["q_lo"], gone(n))
                            split_product(ps[:, 3 * i, 0:SN], lambda a, k: WQ[:, a, k, bass.ds(g * P, P)], x_).then_inc(s["q_mm"], 1)
                            pe.wait_ge(s["k_lo"], gone(n))
                            split_product(ps[:, 3 * i + 1, 0:SN], lambda a, k: WQ[:, a, k, bass.ds(g * P + C, P)],
                                          lambda b, k: raster(x_(b, k))).then_inc(s["k_mm"], 1)
                            pe.wait_ge(s["v_sb"], gone(n))
                            for b_ in range(TPS):
                                last = split_product(ps[:, 3 * i + 2, P * b_:P * (b_ + 1)],
                                                     lambda a, k: xh(img, a, k, m * (2 * SN) + (i * SN + b_ * P), P),
                                                     lambda b, k: WQ[:, b, k, bass.ds(g * P + 2 * C, P)])
                            last.then_inc(s["v_mm"], 1)
                    strips = pe.snap(st * STRIPS + STRIPS + CREDIT)
                    for name in ("q_lo", "k_lo", "v_sb"):
                        pe.wait_ge(s[name], strips)
                    for name in ("q_in", "k_in"):
                        pe.wait_ge(s[name], st * (3 * 48) + (2 * 48 + CREDIT))
                    pe.wait_ge(s["krs_in"], 48)
                    pe.wait_ge(s["vreg_in"], st * 32 + 32)
                    pe.wait_ge(s["kpad"], 1)
                    pe.wait_ge(s["gn_lo"], IMAGES * GN_STEPS)
                    for h in range(HEADS):
                        scores(0, 0, pe.snap(st * TILES), g, h, 0, 0)

                    def step(i, m, tile0, pair0):
                        for b in range(TPS):
                            t = 3 * i + b
                            nxt = None
                            if t < TILES - 1:
                                a1 = i + (b + 1) // TPS
                                if a1 == 0 or a1 == 5:
                                    row0 = 0 if a1 == 0 else LAST0
                                else:
                                    row0 = pe.snap(m * (2 * TR) + (a1 * TR - 3)) if not isinstance(m, int) else a1 * TR - 3
                                nxt = (row0, (b + 1) % TPS)
                            if i == 2 and b == 0:
                                for name in ("q_in", "k_in"):
                                    pe.wait_ge(s[name], st * (3 * 48) + (3 * 48 + CREDIT))
                            for h in range(HEADS):
                                transposes(t, tile0, h)
                                if nxt:
                                    scores(t + 1, m, tile0, g, h, *nxt)
                                if h and t:
                                    values(t - 1, tile0, pair0, h - 1)
                    strip_walk(pe, st, step)
                    for c in range(3):
                        values(TILES - 1, pe.snap(st * TILES), pe.snap(st * (TILES // 2)), c)
                    counted(pe, s["osplit"], st * TILES + TILES + CREDIT)
                    with pe.Fori(0, STRIPS // 2) as m:
                        for i in (0, 1):
                            n = pe.snap(st * STRIPS + m * 2 + i)
                            pe.wait_ge(s["op_done"], gone(n))
                            for j in range(KC):
                                last = split_product(ps[:, 3 * i + j, 0:SN],
                                                     lambda a, k: WO[:, a, :, :].rearrange("p k n -> p (k n)")[:, bass.ds(g * C + j * P, P)],
                                                     lambda b, k: OS[:, bass.ds(m * (2 * SN) + (i * SN + b * N), SN)], steps=1)
                            last.then_inc(s["op_mm"], 1)
            pe.wait_ge(s["c2_in"], 16)
            pe.wait_ge(s["op_done"], STAGES * STRIPS + CREDIT)
            pe.wait_ge(s["flo"], 4)
            pe.wait_ge(s["id16_in"], 16)
            with pe.Fori(0, IMAGES) as img:
                pe.wait_ge(s["y_done"], img * (STRIPS * KC) + CREDIT)
                group_means(pe.snap(img + IMAGES), G2)
                counted(pe, s["gn_lo"], img * GN_STEPS + (IMAGES + 1) * GN_STEPS)
                with pe.Fori(0, TILES) as t:
                    last = split_product(ps[:, 7, bass.ds(t * EXPERTS, EXPERTS)], lambda a, k: xh(img, a, k, t * P, P),
                                         lambda b, k: RWs[:, b, k, :])
                    last.then_inc(s["lg_mm"], 1)

                def hidden(i, n, a):
                    for b in range(TPS):
                        t = 3 * i + b
                        pe.wait_ge(s["cx_cs"], n * TPS + b + 1)
                        if b == 0:
                            pe.wait_ge(s["hf"], n * KC + CREDIT)
                            pe.wait_ge(s["ct_sb"], start(n))
                        for j in range(KC):
                            nc.tensor.transpose(ps[:, 2 + j, b * P:(b + 1) * P], CX[:, t % 2, j * P:(j + 1) * P], ID[:, :])
                        nc.tensor.transpose(ct_bank[:, b * P:(b + 1) * P], CS[:, t % 2, :], ID16).then_inc(s["cb_mm"], 1)
                    a_ = a
                    for k_ in range(KC):
                        u = (3 * i + k_) % 2
                        pe.wait_ge(s["ge"], gone(n * KC + k_))
                        split_product(ps[:, u, 0:SN], lambda a, k: W1[:, a, k, k_ * P:(k_ + 1) * P],
                                      lambda b, k: xh(img, b, k, a_ * SN, SN)).then_inc(s["h_mm"], 1)

                def result(i, n, a):
                    pe.wait_ge(s["hl"], n * KC + KC + CREDIT)
                    pe.wait_ge(s["hh"], n * KC + KC)
                    pe.wait_ge(s["ct_sb"], done(n))
                    for j in range(KC):
                        bank = ps[:, 6 + (3 * i + j) % 2, 0:SN]
                        pe.wait_ge(s["y_done"], gone(n * KC + j))
                        split_product(bank, lambda a, k: W2[:, a, k, j * P:(j + 1) * P],
                                      lambda b, k: HW[:, i % 2, b, k, :], finish=False)
                        mm(bank, B2[0:96, j * P:(j + 1) * P], CT[0:96, i % 2, :], start=False, stop=True).then_inc(s["y_mm"], 1)

                expert_walk(pe, img, hidden, result)


def tile_masks():
    import numpy as np

    def near(size, tile, region, first, start):
        q = first + np.arange(tile)
        w = np.clip(q - WIN // 2, 0, size - WIN)[:, None]
        k = start + np.arange(region)[None, :]
        return (k >= w) & (k < w + WIN)

    rows = [near(H, TR, RR, 0, 0), near(H, TR, RR, TR, TR - 3), near(H, TR, RR, H - TR, LAST0)]
    cols = [near(W, TC, RC, TC * b, 13 * b) for b in range(TPS)]
    out = np.zeros((9, P, KEYS), np.float32)
    for a in range(3):
        for b in range(3):
            ok = rows[a][:, None, :, None] & cols[b][None, :, None, :]
            out[3 * a + b, :, :RK] = np.where(ok.reshape(P, RK), 0.0, -1e30)
    return (out.view(np.uint32) >> 16).astype(np.uint16)


def kernel(x, L0_conv_registers, L0_conv_qkv_w, L0_conv_qkv_b, L0_conv_out_w, L0_conv_out_b, L1_conv_router_w,
           L1_conv_router_b, L1_conv_fc1_w, L1_conv_fc1_b, L1_conv_fc2_w, L1_conv_fc2_b):
    import numpy as np
    import concourse.bacc as bacc
    from concourse.bass_utils import run_bass_kernel_spmd

    def rows(w):
        w = np.asarray(w)
        return np.ascontiguousarray(w.reshape(-1, P, w.shape[-1]).transpose(1, 0, 2))

    def flat(w):
        w = rows(w)
        return w.reshape(P, -1)

    def column(b):
        return np.ascontiguousarray(np.asarray(b).reshape(-1, P).T)

    x = np.asarray(x)
    xc = x.reshape(IMAGES, STRIPS, TR, TPS, TC, KC, P).transpose(0, 6, 5, 1, 3, 2, 4).reshape(IMAGES, P, KC, N)
    qkv_b = np.asarray(L0_conv_qkv_b)
    group = np.arange(C) // (C // GROUPS)
    gmat = (group[:, None] == group[None, :]).astype(np.float32) / np.float32(C // GROUPS)
    tri = np.broadcast_to(np.tril(np.ones((EXPERTS, EXPERTS), np.float32), -1).reshape(1, -1), (P, EXPERTS ** 2))
    arrays = {
        "x": np.ascontiguousarray(xc),
        "wqkv": flat(np.asarray(L0_conv_qkv_w).T), "wo": flat(np.asarray(L0_conv_out_w).T),
        "fc1": flat(np.asarray(L1_conv_fc1_w).reshape(EXPERTS * HID, C).T),
        "fc2": flat(np.asarray(L1_conv_fc2_w).transpose(0, 2, 1).reshape(EXPERTS * HID, C)),
        "rw": flat(np.asarray(L1_conv_router_w).T), "regs": flat(np.asarray(L0_conv_registers).T),
        "qkb": column(qkv_b[:2 * C]), "bv": np.ascontiguousarray(qkv_b[2 * C:]), "ob": column(L0_conv_out_b),
        "fb1": column(np.asarray(L1_conv_fc1_b).reshape(-1)), "fb2": np.ascontiguousarray(L1_conv_fc2_b),
        "rb": np.ascontiguousarray(L1_conv_router_b), "masks": tile_masks(),
        "gmat": rows(gmat), "ident": np.eye(P, dtype=np.float32), "ident16": np.eye(P, dtype=np.float16),
        "tri": np.ascontiguousarray(tri),
    }
    nc = bacc.Bacc("TRN2", target_bir_lowering=False, num_devices=1)
    aps = {n: nc.dram_tensor(f"in_{n}", a.shape, mybir.dt.from_np(a.dtype), kind="ExternalInput").ap() for n, a in arrays.items()}
    out = nc.dram_tensor("out", (IMAGES, P, KC, N), F32, kind="ExternalOutput").ap()
    build(nc, out=out, **aps)
    r = run_bass_kernel_spmd(nc, [{f"in_{n}": a for n, a in arrays.items()}], core_ids=[0])
    y = np.asarray(r.results[0]["out"])
    return np.ascontiguousarray(
        y.reshape(IMAGES, P, KC, STRIPS, TPS, TR, TC).transpose(0, 3, 5, 4, 6, 2, 1).reshape(IMAGES, H, W, C))
```

```python
import concourse.bass as bass
import concourse.mybir as mybir
from contextlib import ExitStack

F32, F16, BF16, U16 = mybir.dt.float32, mybir.dt.float16, mybir.dt.bfloat16, mybir.dt.uint16
ALU, ACT = mybir.AluOpType, mybir.ActivationFunctionType
AX = mybir.AxisListType.X

IMAGES, H, W, C = 2, 48, 48, 384
N = H * W
P = 128
KC = C // P
HEADS, DH = 4, 32
REGS = 16
WIN = 7
TR, TC = 8, 16
STRIPS, TPS = H // TR, W // TC
TILES = STRIPS * TPS
SN = TPS * P
RR, RC = TR + WIN - 1, TC + WIN - 1
RK = RR * RC
KEYS = RK + REGS
ROWS = (5, 5, 4)
LEN = (5 * RC, 5 * RC, 4 * RC + REGS)
AT = (0, 5 * RC, 10 * RC)
GROUPS, EPS = 32, 1e-5
WS = 16.0
SCORE = DH ** -0.5 / WS ** 2
EXPERTS, HID = 4, 96
LAST0 = H - TR - 3
PADROWS = LAST0 + RR - H
KPAD = PADROWS * W
STAGES = IMAGES * KC
GCH = 2 * SN
GN_STEPS = KC * (N // GCH)
LO_V, LO_P = GN_STEPS // 3, 2 * GN_STEPS // 3


def build(nc, x, wqkv, wo, fc1, fc2, rw, regs, qkb, bv, ob, fb1, fb2, rb, masks, gmat, ident, ident16, tri, pick, out):
    ctx = ExitStack()
    with ctx:
        sb = lambda name, shape, dt=F32: ctx.enter_context(nc.sbuf_tensor(name, shape, dt))
        sem = lambda name: ctx.enter_context(nc.semaphore(name))

        X = sb("X", [P, IMAGES * KC * N])
        XH = sb("XH", [P, IMAGES * 2 * KC * N], F16)
        QS = sb("QS", [P, HEADS * N], F16)
        KS = sb("KS", [P, HEADS * N + KPAD], F16)
        KRS = sb("KRS", [P, HEADS, KC, REGS], F16)
        WQ = sb("WQ", [P, 2, KC, 3 * C], F16)
        WO = sb("WO", [P, 2, KC, C], F16)
        OS = sb("OS", [P, 2 * N], F16)
        PT = sb("PT", [P, 2, HEADS, C])
        PR = sb("PR", [P, 2, KEYS])
        VR = sb("VR", [P, 2, 3, P])
        MK = sb("MK", [P, 2, TPS, KEYS], U16)
        O32 = sb("O32", [P, 2, P])
        RX = sb("RX", [P, 2, P])
        RB = sb("RB", [P, 2, P])
        ID = sb("ID", [P, P])
        QT = sb("QT", [P, 2, 2, SN], F16)
        KT = sb("KT", [P, 2, 2, SN], F16)
        VT = sb("VT", [P, 2, TPS, P])
        BV = sb("BV", [P, C])
        KR = sb("KR", [P, 2, KC, REGS], F16)
        RG = sb("RG", [P, 2, KC, REGS], F16)
        SM = sb("SM", [P, 116])
        ps = ctx.enter_context(nc.psum_tensor("ps", [P, 8, 512], F32))

        cols, at = {}, 0
        for name, n in (("qkb", 6), ("qkb16", 6), ("ob", 3), ("fb1", 3), ("rb", 4), ("mv", 6), ("sq", 3),
                        ("gs", 6), ("var", 3), ("sd", 3), ("rstd", 3), ("nb", 3), ("negm", 8), ("rs", 8), ("ri", 8), ("warm", 1), ("credit", 42)):
            cols[name] = SM[:, at:at + n]
            at += n
        assert at <= 116
        negm = cols["negm"].rearrange("p (t h) -> p t h", t=2)
        rs = cols["rs"].rearrange("p (t h) -> p t h", t=2)
        ri = cols["ri"].rearrange("p (t h) -> p t h", t=2)
        mv = cols["mv"].rearrange("p (c s) -> p c s", s=2)
        gs = cols["gs"].rearrange("p (c s) -> p c s", s=2)

        wraw = QS[:, 0:2 * 3 * KC * C].bitcast(F32)
        oraw = KS[:, 0:2 * KC * C].bitcast(F32)
        rraw = KS[:, 2 * KC * C:2 * KC * C + 2 * KC * REGS].bitcast(F32)
        vreg_sb = KS[:, 4096:4096 + 2 * C].bitcast(F32)
        ptf = PT[:, :, :, :].rearrange("p a h n -> p (a h n)")
        gtmp = OS[:, :].bitcast(F32).rearrange("p (t n) -> p t n", t=3)
        G = ptf[:, 2 * GCH:2 * GCH + KC * C].rearrange("p (k n) -> p k n", k=KC)
        st6 = O32[:, :, :].rearrange("p t n -> p (t n)")[:, 0:KC * STRIPS * 6].rearrange("p (c s e) -> p c s e", c=KC, e=6)
        fcw = WQ[:, :, :, :].rearrange("p s k n -> p (s k n)")
        W1 = fcw[:, 0:2 * KC * C].rearrange("p (s k n) -> p s k n", s=2, k=KC)
        W2 = fcw[:, 2 * KC * C:4 * KC * C].rearrange("p (s k n) -> p s k n", s=2, k=KC)
        RWs = fcw[:, 4 * KC * C:4 * KC * C + 2 * KC * EXPERTS].rearrange("p (s k n) -> p s k n", s=2, k=KC)
        f1raw = QS[:, 0:2 * KC * C].bitcast(F32)
        f2raw = QS[:, 2 * KC * C:4 * KC * C].bitcast(F32)
        rwraw = QS[:, 4 * KC * C:4 * KC * C + 2 * KC * EXPERTS].bitcast(F32)
        b2raw = QS[:, 4 * KC * C + 64:4 * KC * C + 64 + 2 * C].bitcast(F32)
        G2 = QS[:, 6 * KC * C:8 * KC * C].bitcast(F32).rearrange("p (k n) -> p k n", k=KC)
        rest = fcw[:, 4 * KC * C + 2 * KC * EXPERTS:]
        B2 = rest[:, 0:C]
        PICK = rest[:, C:2 * C]
        ID16 = rest[:, 2 * C:2 * C + P]
        HW = ptf.bitcast(F16)[:, 0:12 * SN].rearrange("p (a s k n) -> p a s k n", a=2, s=2, k=KC)
        k32 = KS[:, 0:4 * 2304].bitcast(F32)
        GE = k32[:, 0:2 * SN].rearrange("p (t n) -> p t n", t=2)
        HF = k32[:, 2 * SN:4 * SN].rearrange("p (t n) -> p t n", t=2)
        r32 = k32[:, 4 * SN:4 * SN + 1024]
        LG = r32[:, 0:72].rearrange("p (t e) -> p t e", e=EXPERTS)
        EX = r32[:, 72:144].rearrange("p (t e) -> p t e", e=EXPERTS)
        SE = r32[:, 144:216].rearrange("p (t e) -> p t e", e=EXPERTS)
        CB = r32[:, 216:288].rearrange("p (t e) -> p t e", e=EXPERTS)
        RK_ = r32[:, 288:360].rearrange("p (t e) -> p t e", e=EXPERTS)
        M1 = r32[:, 360:378]
        ZS = r32[:, 378:396]
        S2 = r32[:, 396:414]
        TRI = r32[:, 416:432].rearrange("p (i j) -> p i j", j=EXPERTS)
        GT = r32[:, 432:720].rearrange("p (t i j) -> p t i j", i=EXPERTS, j=EXPERTS)
        EQ = r32[:, 720:1008].rearrange("p (t i j) -> p t i j", i=EXPERTS, j=EXPERTS)
        ks16 = KS[:, 2 * (4 * SN + 1024):]
        CT = ks16[:, 0:N]
        CS = ks16[:, N:N + TILES * 96].rearrange("p (t n) -> p t n", t=TILES)

        vscr = nc.dram_tensor("vscr", [N + PADROWS * W, P], F32, kind="Internal").ap()
        vrscr = nc.dram_tensor("vrscr", [REGS, C], F32, kind="Internal").ap()
        qkscr = nc.dram_tensor("qkscr", [2, 2, P, N], F16, kind="Internal").ap()
        krscr = nc.dram_tensor("krscr", [2, P, KC * REGS], F16, kind="Internal").ap()
        v_rows = vscr.rearrange("(r c) d -> r c d", c=W)
        v_tiles = vscr[0:N, :].rearrange("(a r b c) d -> a b r c d", r=TR, b=TPS, c=TC)

        xs = lambda img, c, n0, n: X[:, bass.ds(img * (KC * N) + c * N + n0, n)]
        xh = lambda img, s, c, n0, n: XH[:, bass.ds(img * (2 * KC * N) + (s * KC + c) * N + n0, n)]
        S_BANK = lambda h: ps[:, h, :]
        T_BANK = lambda i: ps[:, 4 + i, :]
        O_BANK = lambda i: ps[:, 6 + i, :]

        names = """w_in wo_in r_in c_in b_in id_in whi wlo wohi wolo rhi rlo b16 kr_mm kr_hi kr_lo vr_mm vr_sb vr_out
            ob_add chain gn_st gn_mm gn_var gn_sd gn_par gn_hi gn_t gn_lo gn_lo_v
            q_mm k_mm v_mm q_hi k_hi q_lo k_lo v_sb q_in k_in kr_out krs_in vreg_in m_inner m_first m_next m_last pv norm ohi osplit rinv rx rbs op_mm op_done
            f_in fhi flo b2_in b2z b2s moe_in lg_mm ex_in ex_out comb csz ct_mm cb_mm ct_sb kpad c2_in
            h_mm ge hf hh hl y_mm y_done y_out""".split()
        s = {n: sem(n) for n in names}
        x_in = [[sem(f"x_in{i}{c}") for c in range(KC)] for i in range(IMAGES)]
        q_out, k_out, v_out, v_in = ([sem(f"{n}{i}") for i in (0, 1)] for n in ("q_out", "k_out", "v_out", "v_in"))
        s_mm, ttr, exd, trd, evd = ([sem(f"{n}{h}") for h in range(HEADS)] for n in ("s_mm", "ttr", "exd", "trd", "evd"))
        CREDIT = 2
        credited = [s[n] for n in ("q_lo", "k_lo", "v_sb", "pv", "norm", "osplit", "op_done", "ge", "hf", "hl",
                                   "y_done", "q_in", "k_in")] + [ttr[3]] + q_out + k_out + v_in + s_mm + exd + trd + evd
        gone = lambda n: n + 1
        done = lambda n: n + 1 + CREDIT
        start = lambda n: n + CREDIT
        V_START = 16
        Y_CREDIT = 2 * KC

        def counted(eng, sem, count, least=1):
            count = eng.to_reg(count)
            eng.wait_ge(sem, least)
            eng.wait_ge(sem, count)

        block = ctx.enter_context(nc.Block())

        def strip_walk(eng, st, body):
            t0, p0 = eng.snap(st * TILES), eng.snap(st * (TILES // 2))
            body(0, 0, t0, p0)
            with eng.Fori(0, 2) as m:
                t1, p1 = eng.snap(st * TILES + m * 6), eng.snap(st * (TILES // 2) + m * 3)
                body(1, m, t1, p1)
                body(2, m, t1, p1)
            t2, p2 = eng.snap(st * TILES), eng.snap(st * (TILES // 2))
            body(5, 0, t2, p2)

        def x_strip(img, a):
            base = X[:, :].rearrange("p (i k n) -> p i k n", i=IMAGES, k=KC)
            return base[:, bass.ds(img, 1), :, bass.ds(a * SN, SN)].rearrange("p i k n -> p (i k) n")

        def expert_walk(eng, img, hidden, result, before_last=None):
            def both(i, m, prior):
                n0 = eng.snap(img * STRIPS + m * 2)
                hidden(i, n0 + i, m * 2 + i)
                if prior and result:
                    result(i - 1, n0 + (i - 1), m * 2 + (i - 1))
            both(0, 0, False)
            with eng.Fori(0, 2) as m:
                both(1, m, True)
                both(2, m, True)
            if before_last:
                with eng.If_eq(eng.to_reg(img), 0):
                    before_last()
            both(5, 0, True)
            if result:
                result(5, eng.snap(img * STRIPS + 5), 5)

        ct_bank = lambda q: ps[0:96, 2 + q, 0:SN].bitcast(F16)
        def flat(t, part):
            return t[:, part, :, :].rearrange("p k n -> p (k n)")

        def region_view(ap):
            return bass.AP(ap.tensor, ap.offset, [list(ap.ap[0]), [W, RR], [1, RC]])

        raster = lambda ap: ap.rearrange("p (b r c) -> p r b c", r=TR, b=TPS)

        @block.sync
        def _(sp):
            for img in range(IMAGES):
                for c in range(KC):
                    sp.dma_start(xs(img, c, 0, N), x[img, :, c, :]).then_inc(x_in[img][c], 16)
                if img == 0:
                    sp.dma_start(wraw, wqkv).then_inc(s["w_in"], 16)
            sp.dma_start(oraw, wo).then_inc(s["wo_in"], 16)
            sp.wait_ge(s["vr_sb"], 1)
            sp.dma_start(vrscr, vreg_sb[0:REGS, :]).then_inc(s["vr_out"], 16)
            sp.wait_ge(s["vr_out"], 16)
            sp.wait_ge(s["kr_lo"], 1)
            sp.dma_start(krscr.rearrange("s p n -> p s n"), KR[:, :, :, :].rearrange("p s k r -> p s (k r)")).then_inc(s["kr_out"], 16)
            sp.wait_ge(s["kr_out"], 16)
            for j, part in enumerate((0, 1, 0)):
                sp.dma_start(KRS[DH * j:DH * (j + 1), :, :, :].rearrange("d h k r -> d h (k r)"),
                             krscr[part].rearrange("(h d) n -> d h n", d=DH)).then_inc(s["krs_in"], 16)
            sp.wait_ge(s["wolo"], 1)
            sp.dma_start(MK[:, 0, :, :], masks[TPS:2 * TPS].rearrange("b p n -> p b n")).then_inc(s["m_inner"], 16)
            with sp.Fori(0, IMAGES) as img:
                with sp.Fori(0, KC) as g:
                    st = sp.snap(img * KC + g)
                    sp.wait_ge(ttr[3], st * TILES + CREDIT)
                    sp.dma_start(MK[:, 1, :, :], masks[0:TPS].rearrange("b p n -> p b n")).then_inc(s["m_first"], 16)
                    sp.wait_ge(s["pv"], st * TILES + CREDIT)
                    for i in (0, 1):
                        sp.dma_start(VR[4 * RC:4 * RC + REGS, i, 2, :], vrscr[:, bass.ds(g * P, P)]).then_inc(s["vreg_in"], 16)
                    for h in range(HEADS):
                        counted(sp, s_mm[h], st * TILES + CREDIT)

                    def pair(m):
                        use = sp.snap(st * (STRIPS // 2) + m)
                        sp.wait_ge(s["q_in"], use * 48 + CREDIT)
                        sp.wait_ge(s["k_in"], use * 48 + CREDIT)
                        for i in (0, 1):
                            n = sp.snap(st * STRIPS + m * 2 + i)
                            for q, (stage, name, full, moved) in enumerate(((QT, "q", q_out, s["q_lo"]), (KT, "k", k_out, s["k_lo"]))):
                                counted(sp, s[name + "_hi"], n + 1)
                                counted(sp, moved, done(n))
                                sp.dma_start(qkscr[q].rearrange("s p n -> p s n")[:, :, bass.ds(m * (2 * SN) + i * SN, SN)],
                                             stage[:, i, :, :]).then_inc(full[i], 16)
                        for q, (stack, full, name, parts) in enumerate(((QS, q_out, "q_in", (0, 0, 1)), (KS, k_out, "k_in", (0, 1, 0)))):
                            for i in (0, 1):
                                counted(sp, full[i], use * 16 + 16 + CREDIT, 16 + CREDIT)
                            for j, part in enumerate(parts):
                                sp.dma_start(stack[DH * j:DH * (j + 1), 0:HEADS * N].rearrange("d (h n) -> d h n", h=HEADS)[
                                                 :, :, bass.ds(m * (2 * SN), 2 * SN)],
                                             qkscr[q, part].rearrange("(h d) n -> d h n", d=DH)[:, :, bass.ds(m * (2 * SN), 2 * SN)]
                                             ).then_inc(s[name], 16)

                    def region(t, row0, tile0):
                        sp.wait_ge(s["pv"], gone(tile0 + t))
                        x0 = 13 * (t % TPS)
                        for c in range(3):
                            sp.dma_start(VR[0:ROWS[c] * RC, t % 2, c, :],
                                         v_rows[bass.ds(row0 + 5 * c, ROWS[c]), x0:x0 + RC, :]).then_inc(v_in[t % 2], 16)

                    def regions(i, m, tile0, pair0):
                        row0 = 0 if i == 0 else LAST0 if i == 5 else sp.snap(m * (2 * TR) + (i * TR - 3))
                        for b in range(TPS):
                            t = TPS * i + b
                            if t >= 2:
                                region(t, row0, tile0)
                        if i == 1:
                            sp.wait_ge(ttr[3], done(tile0 + TPS))
                            sp.dma_start(MK[:, 1, 0, :], masks[bass.ds(m * TPS + TPS, 1)].rearrange("a p n -> (a p) n")).then_inc(s["m_next"], 16)
                        if i == 0:
                            sp.wait_ge(ttr[3], done(tile0 + (TPS - 1)))
                            sp.dma_start(MK[:, 1, 1:TPS, :], masks[2 * TPS + 1:3 * TPS].rearrange("b p n -> p b n")).then_inc(s["m_last"], 16)

                    with sp.If_eq(sp.to_reg(g), 1):
                        sp.dma_start(G, gmat).then_inc(s["c2_in"], 16)
                    with sp.Fori(0, STRIPS // 2 - 1) as m:
                        pair(m)
                    for i in (0, 1):
                        counted(sp, v_out[i], st * (3 * 48) + (2 * 48 + V_START), 2 * 48 + V_START)
                    for t in (0, 1):
                        region(t, 0, sp.snap(st * TILES))
                    pair(STRIPS // 2 - 1)
                    for i in (0, 1):
                        counted(sp, v_out[i], st * (3 * 48) + (3 * 48 + V_START), 3 * 48 + V_START)
                    strip_walk(sp, st, regions)
            sp.wait_ge(s_mm[3], STAGES * TILES + CREDIT)
            for src, dst in ((fc1, f1raw), (fc2, f2raw), (rw, rwraw)):
                sp.dma_start(dst, src).then_inc(s["f_in"], 16)
            for j in range(3):
                sp.dma_start(b2raw[DH * j:DH * j + EXPERTS, :], fb2).then_inc(s["b2_in"], 16)
            for src, dst in ((tri, TRI.rearrange("p i j -> p (i j)")), (ident16, ID16), (pick, PICK[0:96, :])):
                sp.dma_start(dst, src).then_inc(s["moe_in"], 16)
            sp.dma_start(G2, gmat).then_inc(s["c2_in"], 16)
            with sp.Fori(0, IMAGES) as img:
                with sp.Fori(0, STRIPS) as a:
                    n = sp.snap(img * STRIPS + a)
                    sp.wait_ge(s["y_done"], n * KC + KC + CREDIT)
                    sp.dma_start(out[bass.ds(img, 1), :, :, bass.ds(a * SN, SN)].rearrange("i p k n -> (i p) k n"),
                                 x_strip(img, a)).then_inc(s["y_out"], 16)
            sp.wait_ge(s["y_out"], 16 * IMAGES * STRIPS)

        @block.gpsimd
        def _(pool):
            nc.gpsimd.memset(KS[:, HEADS * N:], 0.0).then_inc(s["kpad"], 1)
            for src, dst, name in ((gmat, G, "c_in"), (regs, rraw, "r_in"), (ident, ID[:, :], "id_in"), (bv.partition_broadcast(P), BV[:, :], "b_in"),
                                   (qkb, cols["qkb"], "b_in"), (ob, cols["ob"], "b_in"), (fb1, cols["fb1"], "b_in"),
                                   (rb.partition_broadcast(P), cols["rb"], "b_in")):
                pool.dma_start(dst, src).then_inc(s[name], 16)

            pool.wait_ge(s["kpad"], 1)
            half = KPAD // 2
            for i in (0, 1):
                pool.dma_start(vscr[N + half * i:N + half * (i + 1), :].rearrange("r d -> (r d)").rearrange("(p n) -> p n", p=P),
                               KS[:, HEADS * N:].bitcast(F32)).then_inc(v_out[i], 16)

            def low_halves(img, n, steps=range(GN_STEPS)):
                for i in steps:
                    if i % 3 == 1:
                        continue
                    c, n0 = i % KC, i // KC * GCH
                    counted(pool, s["gn_t"], n * GN_STEPS + i + 1)
                    pool.wait_ge(s["gn_hi"], n * GN_STEPS + i + 1)
                    nc.gpsimd.tensor_tensor(xh(img, 1, c, n0, GCH), gtmp[:, i % 3, :], xh(img, 0, c, n0, GCH),
                                            ALU.subtract).then_inc(s["gn_lo"], 1)

            low_halves(0, 0)

            def attention(img, g):
                st = pool.snap(img * KC + g)
                for i in (0, 1):
                    counted(pool, v_in[i], st * (TILES // 2 * 48) + CREDIT)

                def v_written(m):
                    for i in (0, 1):
                        n = pool.snap(st * STRIPS + m * 2 + i)
                        counted(pool, s["v_sb"], done(n))
                        for b in range(TPS):
                            pool.dma_start(v_tiles[bass.ds(m * 2 + i, 1), b].rearrange("a r c d -> (a r) c d"),
                                           VT[:, i, b, :]).then_inc(v_out[i], 16)

                with pool.If_eq(pool.to_reg(g), 2):
                    low_halves(pool.snap(1 - img), pool.snap(img + 1), range(3, 6))
                with pool.Fori(0, STRIPS // 2 - 1) as m:
                    v_written(m)
                with pool.If_eq(pool.to_reg(g), 1):
                    low_halves(pool.snap(1 - img), pool.snap(img + 1), range(3))
                    counted(pool, s["gn_lo_v"], img * LO_V + (LO_V + 1))
                    pool.wait_ge(s["gn_lo"], img * LO_P + (LO_P + 2))
                with pool.If_eq(pool.to_reg(g), 2):
                    low_halves(pool.snap(1 - img), pool.snap(img + 1), range(6, GN_STEPS))
                    counted(pool, s["gn_lo_v"], img * LO_V + 2 * LO_V)
                    pool.wait_ge(s["gn_lo"], img * LO_P + 2 * LO_P)
                v_written(STRIPS // 2 - 1)

                def split(t, n0, tile0):
                    counted(pool, s["norm"], done(tile0 + t))
                    hi, lo = OS[:, bass.ds(n0, P)], OS[:, bass.ds(n0 + N, P)]
                    nc.gpsimd.tensor_copy(hi, O32[:, t % 2, :]).then_inc(s["ohi"], 1)
                    pool.wait_ge(s["ohi"], tile0 + t + 1)
                    nc.gpsimd.tensor_tensor(lo, O32[:, t % 2, :], hi, ALU.subtract).then_inc(s["osplit"], 1)

                def step(i, m, tile0, pair0):
                    for b in range(TPS):
                        t = 3 * i + b
                        counted(pool, s["pv"], gone(tile0 + t))
                        counted(pool, s["rinv"], tile0 + t + 1)
                        nc.gpsimd.tensor_copy(RX[:, t % 2, :].rearrange("p (h d) -> p h d", h=HEADS),
                                              ri[:, t % 2, :].unsqueeze(2).broadcast_to([P, HEADS, DH])).then_inc(s["rx"], 1)
                        if t >= 2:
                            split(t - 2, pool.snap(m * (2 * SN) + (t - 2) * P), tile0)
                strip_walk(pool, st, step)
                for t in (TILES - 2, TILES - 1):
                    split(t, t * P, pool.snap(st * TILES))
            with pool.Fori(0, IMAGES) as img:
                with pool.Fori(0, KC) as g:
                    attention(img, g)
            pool.wait_ge(s_mm[3], STAGES * TILES + CREDIT)
            nc.gpsimd.memset(B2, 0.0).then_inc(s["b2z"], 1)
            nc.gpsimd.memset(CS, 0.0).then_inc(s["csz"], 1)
            low_halves(1, IMAGES + 1)
            with pool.Fori(0, IMAGES * STRIPS // 2) as m:
                for i in (0, 1):
                    for k in range(KC):
                        unit = pool.snap(m * (2 * KC) + (i * KC + k))
                        pool.wait_ge(s["hf"], done(unit))
                        pool.wait_ge(s["hh"], unit + 1)
                        nc.gpsimd.tensor_tensor(HW[:, i, 1, k, :], HF[:, (i * KC + k) % 2, :], HW[:, i, 0, k, :],
                                                ALU.subtract).then_inc(s["hl"], 1)

        @block.vector
        def _(dve):
            V = nc.vector
            for i, x_ in enumerate(credited):
                V.memset(cols["credit"][:, i:i + 1], 0.0).then_inc(x_, CREDIT)
            V.memset(cols["credit"][:, 41:42], 0.0).then_inc(s["y_mm"], Y_CREDIT)

            def chain(base):
                k = [0]

                def link(ins):
                    k[0] += 1
                    ins.then_inc(s["chain"], 1)
                    counted(dve, s["chain"], base + k[0])
                return link, k

            def statistics(img, n, link, first=False):
                for c in range(KC):
                    if first:
                        dve.wait_ge(x_in[0][c], 16)
                    last = block_statistics(img, c)
                link(last)
                for c in range(KC):
                    last = V.bn_aggr(mv[:, c, :], st6[:, c, :, :].rearrange("p s e -> p (s e)"))
                link(last)
                mean_square(link)

            def block_statistics(img, c):
                for j in range(STRIPS):
                    last = V.bn_stats(st6[:, c, j, :], xs(img, c, j * SN, SN))
                return last

            def spread_statistics(img, c, link):
                link(block_statistics(img, c))
                link(V.bn_aggr(mv[:, c, :], st6[:, c, :, :].rearrange("p s e -> p (s e)")))

            def mean_square(link):
                link(V.tensor_tensor(cols["sq"], mv[:, :, 0], mv[:, :, 0], ALU.mult))
                V.tensor_tensor(mv[:, :, 1], mv[:, :, 1], cols["sq"], ALU.add).then_inc(s["gn_st"], 1)

            def parameters(n, link):
                dve.wait_ge(s["gn_mm"], n + 1)
                link(V.tensor_copy(cols["gs"], ps[:, 7, 0:2 * KC]))
                link(V.tensor_tensor(cols["sq"], gs[:, :, 0], gs[:, :, 0], ALU.mult))
                V.scalar_tensor_tensor(out=cols["var"], in0=gs[:, :, 1], scalar=EPS, in1=cols["sq"],
                                       op0=ALU.add, op1=ALU.subtract).then_inc(s["gn_var"], 1)
                dve.wait_ge(s["gn_sd"], n + 1)
                link(V.reciprocal(cols["rstd"], cols["sd"]))
                V.scalar_tensor_tensor(out=cols["nb"], in0=gs[:, :, 0], scalar=-1.0, in1=cols["rstd"],
                                       op0=ALU.mult, op1=ALU.mult).then_inc(s["gn_par"], 1)
                dve.wait_ge(s["gn_par"], n + 1)

            def normalised(img, n, steps):
                for i in steps:
                    c, n0 = i % KC, i // KC * GCH
                    if not (isinstance(n, int) and n * GN_STEPS + i < 3):
                        counted(dve, *((s["gn_lo"], n * LO_P + i // 3 * 2 - 1), (s["gn_lo_v"], n * LO_V + i // 3),
                                       (s["gn_lo"], n * LO_P + i // 3 * 2))[i % 3])
                    V.tensor_scalar(gtmp[:, i % 3, :], xs(img, c, n0, GCH), cols["rstd"][:, c:c + 1],
                                    cols["nb"][:, c:c + 1], ALU.mult, ALU.add).then_inc(s["gn_t"], 1)
                    if i % 3 == 2:
                        j, c = i - 1, (i - 1) % KC
                        counted(dve, s["gn_hi"], n * GN_STEPS + (j + 1))
                        counted(dve, s["gn_t"], n * GN_STEPS + (j + 1))
                        V.tensor_tensor(xh(img, 1, c, n0, GCH), gtmp[:, 1, :], xh(img, 0, c, n0, GCH),
                                        ALU.subtract).then_inc(s["gn_lo_v"], 1)

            STAT_LINKS = 3
            GN_LINKS = STAT_LINKS + 3
            link, k = chain(0)
            statistics(0, 0, link, first=True)
            dve.wait_ge(s["r_in"], 16)
            dve.wait_ge(s["rhi"], 1)
            V.tensor_tensor(flat(RG, 1), rraw, flat(RG, 0), ALU.subtract).then_inc(s["rlo"], 1)
            dve.wait_ge(s["w_in"], 16)

            def weights_low(j):
                dve.wait_ge(s["whi"], j + 1)
                V.scalar_tensor_tensor(out=WQ[:, 1, j, :], in0=wraw[:, j * 3 * C:(j + 1) * 3 * C], scalar=WS, in1=WQ[:, 0, j, :],
                                       op0=ALU.mult, op1=ALU.subtract).then_inc(s["wlo"], 1)

            weights_low(0)
            parameters(0, link)
            assert k[0] == GN_LINKS
            normalised(0, 0, range(3))
            weights_low(1)
            weights_low(2)
            normalised(0, 0, range(3, GN_STEPS))
            dve.wait_ge(s["b_in"], 16 * 5)
            V.tensor_scalar(cols["qkb16"], cols["qkb"], WS, None, ALU.mult).then_inc(s["b16"], 1)
            dve.wait_ge(s["kr_hi"], 1)
            dve.wait_ge(s["b16"], 1)
            for g in range(KC):
                last = V.scalar_tensor_tensor(out=KR[:, 1, g, :], in0=ps[:, 6, REGS * g:REGS * (g + 1)],
                                              scalar=cols["qkb16"][:, KC + g:KC + g + 1], in1=KR[:, 0, g, :],
                                              op0=ALU.add, op1=ALU.subtract)
            last.then_inc(s["kr_lo"], 1)
            dve.wait_ge(s["vr_mm"], 1)
            V.scalar_tensor_tensor(out=vreg_sb[0:REGS, :], in0=ps[0:REGS, 7, 0:C], scalar=1 / WS, in1=BV[0:REGS, :],
                                   op0=ALU.mult, op1=ALU.add).then_inc(s["vr_sb"], 1)
            dve.wait_ge(s["wo_in"], 16)
            dve.wait_ge(s["wohi"], 1)
            V.scalar_tensor_tensor(out=flat(WO, 1), in0=oraw, scalar=WS, in1=flat(WO, 0), op0=ALU.mult,
                                   op1=ALU.subtract).then_inc(s["wolo"], 1)

            def maxima(t, tile0, mask, heads):
                p = t % 2
                for h in heads:
                    counted(dve, s_mm[h], done(tile0 + t))
                    V.tensor_tensor_reduce(out=S_BANK(h)[:, 0:KEYS], in0=S_BANK(h)[:, 0:KEYS], in1=mask.bitcast(BF16),
                                           scale=-SCORE, scalar=3e38, op0=ALU.add, op1=ALU.min,
                                           accum_out=negm[:, p, h:h + 1]).then_inc(ttr[h], 1)

            def keys_out(t, tile0, h):
                dve.wait_ge(trd[h], done(tile0 + t))
                V.tensor_copy(PT[:, t % 2, h, :], T_BANK(h % 2)[:, 0:C]).then_inc(evd[h], 1)

            def normalise(t, tile0):
                p = t % 2
                dve.wait_ge(s["rbs"], tile0 + t + 1)
                dve.wait_ge(s["osplit"], gone(tile0 + t))
                V.tensor_tensor(O32[:, p, :], O_BANK(p)[:, 0:P], RB[:, p, :], ALU.mult).then_inc(s["norm"], 1)

            with dve.Fori(0, IMAGES) as img:
                with dve.Fori(0, KC) as g:
                    st = dve.snap(img * KC + g)
                    other = dve.snap(1 - img)
                    SPREAD = 2 * KC + 4
                    links = lambda first: chain(dve.snap(img * SPREAD + (GN_LINKS + first)))[0]

                    def block(c):
                        dve.wait_ge(x_in[1][c], 16)
                        counted(dve, s["osplit"], st * TILES + CREDIT)
                        counted(dve, s["op_done"], st * STRIPS + CREDIT)
                        spread_statistics(other, c, links(2 * c))
                    def bias_added(c):
                        counted(dve, s["op_done"], st * STRIPS + CREDIT)
                        counted(dve, s["gn_t"], img * GN_STEPS + GN_STEPS)
                        counted(dve, s["gn_hi"], img * GN_STEPS + GN_STEPS)
                        V.tensor_scalar(xs(img, c, 0, N), xs(img, c, 0, N), cols["ob"][:, c:c + 1], None, ALU.add
                                        ).then_inc(s["ob_add"], 1)

                    with dve.If_eq(dve.to_reg(g), 0):
                        block(0)
                    with dve.If_eq(dve.to_reg(g), 1):
                        block(2)
                        mean_square(links(2 * KC))
                        bias_added(1)
                    with dve.If_eq(dve.to_reg(g), 2):
                        counted(dve, s["op_done"], st * STRIPS + CREDIT)
                        normalised(other, dve.snap(img + 1), range(3, 6))

                    def projected(m, i, last=False):
                        n = dve.snap(st * STRIPS + m * 2 + i)
                        use = dve.snap(st * (STRIPS // 2) + m)
                        dve.wait_ge(s["q_hi"], n + 1)
                        dve.wait_ge(q_out[i], use * 16 + CREDIT)
                        V.scalar_tensor_tensor(out=QT[:, i, 1, :], in0=ps[:, 3 * i, 0:SN],
                                               scalar=cols["qkb16"][:, bass.ds(g, 1)], in1=QT[:, i, 0, :],
                                               op0=ALU.add, op1=ALU.subtract).then_inc(s["q_lo"], 1)
                        if last:
                            dve.wait_ge(s["m_inner"], 16)
                            dve.wait_ge(s["m_first"], st * 16 + 16)
                            maxima(0, dve.snap(st * TILES), MK[:, 1, 0, :], (0,))
                        dve.wait_ge(s["k_hi"], n + 1)
                        dve.wait_ge(k_out[i], use * 16 + CREDIT)
                        V.scalar_tensor_tensor(out=KT[:, i, 1, :], in0=ps[:, 3 * i + 1, 0:SN],
                                               scalar=cols["qkb16"][:, bass.ds(g + KC, 1)], in1=KT[:, i, 0, :],
                                               op0=ALU.add, op1=ALU.subtract).then_inc(s["k_lo"], 1)
                        if last:
                            maxima(0, dve.snap(st * TILES), MK[:, 1, 0, :], (1, 2))
                        dve.wait_ge(s["v_mm"], n + 1)
                        dve.wait_ge(v_out[i], use * 48 + V_START)
                        V.scalar_tensor_tensor(out=VT[:, i, :, :], in0=ps[:, 3 * i + 2, 0:SN].rearrange("p (b n) -> p b n", b=TPS),
                                               scalar=1 / WS, in1=BV[:, bass.ds(g * P, P)].unsqueeze(1).broadcast_to([P, TPS, P]),
                                               op0=ALU.mult, op1=ALU.add).then_inc(s["v_sb"], 1)
                        if last:
                            maxima(0, dve.snap(st * TILES), MK[:, 1, 0, :], (3,))

                    with dve.Fori(0, STRIPS // 2 - 1) as m:
                        projected(m, 0)
                        projected(m, 1)
                    with dve.If_eq(dve.to_reg(g), 0):
                        block(1)
                        bias_added(0)
                    with dve.If_eq(dve.to_reg(g), 1):
                        parameters(dve.snap(img + 1), links(2 * KC + 1))
                        normalised(other, dve.snap(img + 1), range(3))
                    with dve.If_eq(dve.to_reg(g), 2):
                        normalised(other, dve.snap(img + 1), range(6, GN_STEPS))
                        bias_added(2)
                    projected(STRIPS // 2 - 1, 0)
                    projected(STRIPS // 2 - 1, 1, last=True)

                    def step(i, m, tile0, pair0):
                        for b in range(TPS):
                            t = 3 * i + b
                            more = t < TILES - 1
                            a1, b1 = divmod(t + 1, TPS)
                            mask = MK[:, 0 if a1 in (1, 2) else 1, b1, :]
                            if a1 == 3:
                                dve.wait_ge(s["m_next"], st * 32 + m * 16 + 16)
                            elif t == TILES - TPS:
                                dve.wait_ge(s["m_last"], st * 16 + 16)
                            if more:
                                maxima(t + 1, tile0, mask, (0,))
                            keys_out(t, tile0, 1)
                            if t >= 2:
                                normalise(t - 2, tile0)
                            if more:
                                maxima(t + 1, tile0, mask, (1, 2))
                            keys_out(t, tile0, 3)
                            if more:
                                maxima(t + 1, tile0, mask, (3,))
                            dve.wait_ge(exd[3], done(tile0 + t))
                            V.reciprocal(ri[:, t % 2, :], rs[:, t % 2, :]).then_inc(s["rinv"], 1)
                    strip_walk(dve, st, step)
                    normalise(TILES - 2, dve.snap(st * TILES))
                    dve.wait_ge(s["ob_add"], st + 1)
                    for a in range(STRIPS):
                        dve.wait_ge(s["op_mm"], st * STRIPS + (a + 1))
                        for j in range(KC):
                            xj = xs(img, j, a * SN, SN)
                            last = V.scalar_tensor_tensor(out=xj, in0=ps[:, 3 * (a % 2) + j, 0:SN], scalar=1 / WS, in1=xj,
                                                          op0=ALU.mult, op1=ALU.add)
                        last.then_inc(s["op_done"], 1)
                        if a == 0:
                            normalise(TILES - 1, dve.snap(st * TILES))
            dve.wait_ge(s["op_done"], STAGES * STRIPS + CREDIT)
            dve.wait_ge(s["osplit"], STAGES * TILES + CREDIT)
            BASE = GN_LINKS + IMAGES * SPREAD
            link, k = chain(BASE)
            dve.wait_ge(s["fhi"], 3)
            for raw, w in ((rwraw, RWs), (f1raw, W1), (f2raw, W2)):
                V.scalar_tensor_tensor(out=flat(w, 1), in0=raw, scalar=WS, in1=flat(w, 0), op0=ALU.mult,
                                       op1=ALU.subtract).then_inc(s["flo"], 1)
            dve.wait_ge(s["b2s"], 1)
            V.scalar_tensor_tensor(out=B2[64:68, :], in0=b2raw[64:68, :], scalar=WS, in1=B2[64:68, :], op0=ALU.mult,
                                   op1=ALU.subtract).then_inc(s["flo"], 1)
            statistics(1, IMAGES + 1, link)
            dve.wait_ge(s["moe_in"], 48)
            dve.wait_ge(s["csz"], 1)
            LINKS = 14

            def router(img):
                link, k = chain(BASE + (LINKS + GN_LINKS if img else STAT_LINKS))
                dve.wait_ge(s["lg_mm"], (img + 1) * (TILES // 6))
                bc = lambda ap: ap.unsqueeze(2).broadcast_to([P, TILES, EXPERTS])
                lg = ps[:, 5, 0:TILES * 2 * EXPERTS].rearrange("p (t b e) -> p t b e", b=2, e=EXPERTS)
                link(V.scalar_tensor_tensor(out=LG, in0=lg[:, :, 1, :], scalar=1 / WS,
                                            in1=cols["rb"].unsqueeze(1).broadcast_to([P, TILES, EXPERTS]),
                                            op0=ALU.mult, op1=ALU.add))
                link(V.scalar_tensor_tensor(out=LG, in0=lg[:, :, 0, :], scalar=1 / WS, in1=LG, op0=ALU.mult, op1=ALU.add))
                link(V.reduce_max(M1, LG, AX))
                V.tensor_tensor(EX, LG, bc(M1), ALU.subtract).then_inc(s["ex_in"], 1)
                pair = [P, TILES, EXPERTS, EXPERTS]
                lj, li = LG.unsqueeze(2).broadcast_to(pair), LG.unsqueeze(3).broadcast_to(pair)
                V.tensor_tensor(GT, lj, li, ALU.is_gt)
                link(V.tensor_tensor(EQ, lj, li, ALU.is_equal))
                link(V.tensor_tensor(EQ, EQ, TRI.unsqueeze(1).broadcast_to(pair), ALU.mult))
                link(V.tensor_tensor(GT, GT, EQ, ALU.add))
                link(V.reduce_sum(RK_, GT, AX))
                link(V.tensor_scalar(RK_, RK_, 1.5, None, ALU.is_lt))
                dve.wait_ge(s["ex_out"], img + 1)
                link(V.tensor_tensor(SE, EX, RK_, ALU.mult))
                V.reduce_sum(ZS, EX, AX)
                link(V.reduce_sum(S2, SE, AX))
                link(V.scalar_tensor_tensor(out=S2, in0=ZS, scalar=1e-8, in1=S2, op0=ALU.mult, op1=ALU.add))
                link(V.reciprocal(S2, S2))
                link(V.tensor_tensor(CB, SE, bc(S2), ALU.mult))
                link(V.tensor_copy(CS[:, :, 0:EXPERTS], CB))
                V.tensor_copy(CS[:, :, 64:64 + EXPERTS], CS[:, :, 0:EXPERTS])
                V.tensor_tensor(CS[:, :, 32:32 + EXPERTS], CB, CS[:, :, 0:EXPERTS], ALU.subtract).then_inc(s["comb"], 1)
                assert k[0] == LINKS

            router(0)
            parameters(IMAGES + 1, chain(BASE + STAT_LINKS + LINKS)[0])
            normalised(1, IMAGES + 1, range(GN_STEPS))
            with dve.Fori(0, IMAGES) as img:
                def weigh(i, n, a):
                    dve.wait_ge(s["cb_mm"], n + 1)
                    for k_ in range(KC):
                        u, unit = (3 * i + k_) % 2, n * KC + k_
                        dve.wait_ge(s["ge"], done(unit))
                        dve.wait_ge(s["hl"], gone(unit))
                        V.tensor_tensor(HF[:, u, :], ps[:, 2 + k_, 0:SN], GE[:, u, :], ALU.mult).then_inc(s["hf"], 1)

                def result(i, n, a):
                    for j in range(KC):
                        xj = xs(img, j, a * SN, SN)
                        dve.wait_ge(s["y_mm"], n * KC + j + 1 + Y_CREDIT)
                        V.scalar_tensor_tensor(out=xj, in0=ps[:, 6 + (3 * i + j) % 2, 0:SN], scalar=1 / WS, in1=xj,
                                               op0=ALU.mult, op1=ALU.add).then_inc(s["y_done"], 1)

                expert_walk(dve, img, weigh, result, lambda: router(1))

        @block.scalar
        def _(act):
            A = nc.scalar.activation

            def deviation(n):
                act.wait_ge(s["gn_var"], n + 1)
                A(cols["sd"], cols["var"], ACT.Sqrt).then_inc(s["gn_sd"], 1)

            def normalised(img, n, steps=range(GN_STEPS)):
                act.wait_ge(s["gn_par"], n + 1)
                for i in steps:
                    c, n0 = i % KC, i // KC * GCH
                    A(xh(img, 0, c, n0, GCH), xs(img, c, n0, GCH), ACT.Identity, bias=cols["nb"][:, c:c + 1],
                      scale=cols["rstd"][:, c:c + 1]).then_inc(s["gn_hi"], 1)

            act.wait_ge(s["q_lo"], CREDIT)
            A(cols["warm"], cols["credit"][:, 0:1], ACT.Sqrt)
            act.wait_ge(s["r_in"], 16)
            A(flat(RG, 0), rraw, ACT.Copy).then_inc(s["rhi"], 1)
            act.wait_ge(s["w_in"], 16)
            for j in range(KC):
                A(WQ[:, 0, j, :], wraw[:, j * 3 * C:(j + 1) * 3 * C], ACT.Copy, scale=WS).then_inc(s["whi"], 1)
            deviation(0)
            normalised(0, 0)
            act.wait_ge(s["kr_mm"], 1)
            act.wait_ge(s["b16"], 1)
            for g in range(KC):
                last = A(KR[:, 0, g, :], ps[:, 6, REGS * g:REGS * (g + 1)], ACT.Identity,
                         bias=cols["qkb16"][:, KC + g:KC + g + 1])
            last.then_inc(s["kr_hi"], 1)
            act.wait_ge(s["wo_in"], 16)
            A(flat(WO, 0), oraw, ACT.Copy, scale=WS).then_inc(s["wohi"], 1)

            def keys_out(t, tile0, h):
                act.wait_ge(trd[h], done(tile0 + t))
                nc.scalar.copy(PT[:, t % 2, h, :], T_BANK(h % 2)[:, 0:C]).then_inc(evd[h], 1)

            def rb_out(t, tile0):
                act.wait_ge(s["pv"], done(tile0 + t))
                nc.scalar.copy(RB[:, t % 2, :], O_BANK(t % 2)[:, P:2 * P]).then_inc(s["rbs"], 1)

            def exps(t, tile0, heads):
                p = t % 2
                for h in heads:
                    act.wait_ge(ttr[h], tile0 + t + 1 + (CREDIT if h == 3 else 0))
                    act.wait_ge(trd[(h + 2) % 4], start(tile0 + t + (1 if h >= 2 else 0)))
                    A(PR[:, h % 2, :], S_BANK(h)[:, 0:KEYS], ACT.Exp, bias=negm[:, p, h:h + 1], scale=-1.0,
                      accum_out=rs[:, p, h:h + 1]).then_inc(exd[h], 1)

            with act.Fori(0, IMAGES) as img:
                with act.Fori(0, KC) as g:
                    st = act.snap(img * KC + g)

                    def projected(m, i):
                        n = act.snap(st * STRIPS + m * 2 + i)
                        use = act.snap(st * (STRIPS // 2) + m)
                        counted(act, s["q_mm"], n + 1)
                        act.wait_ge(q_out[i], use * 16 + CREDIT)
                        A(QT[:, i, 0, :], ps[:, 3 * i, 0:SN], ACT.Identity, bias=cols["qkb16"][:, bass.ds(g, 1)]
                          ).then_inc(s["q_hi"], 1)
                        counted(act, s["k_mm"], n + 1)
                        act.wait_ge(k_out[i], use * 16 + CREDIT)
                        A(KT[:, i, 0, :], ps[:, 3 * i + 1, 0:SN], ACT.Identity,
                          bias=cols["qkb16"][:, bass.ds(g + KC, 1)]).then_inc(s["k_hi"], 1)

                    with act.If_eq(act.to_reg(g), 2):
                        normalised(act.snap(1 - img), act.snap(img + 1), range(3, 6))
                    with act.Fori(0, STRIPS // 2 - 1) as m:
                        projected(m, 0)
                        projected(m, 1)
                    with act.If_eq(act.to_reg(g), 1):
                        deviation(act.snap(img + 1))
                        normalised(act.snap(1 - img), act.snap(img + 1), range(3))
                    with act.If_eq(act.to_reg(g), 2):
                        normalised(act.snap(1 - img), act.snap(img + 1), range(6, GN_STEPS))
                    A(cols["warm"], cols["ob"][:, 0:1], ACT.Exp)
                    projected(STRIPS // 2 - 1, 0)
                    projected(STRIPS // 2 - 1, 1)
                    exps(0, act.snap(st * TILES), (0,))

                    def step(i, m, tile0, pair0):
                        for b in range(TPS):
                            t = 3 * i + b
                            exps(t, tile0, (1,))
                            if t >= 2:
                                rb_out(t - 2, tile0)
                            keys_out(t, tile0, 0)
                            exps(t, tile0, (2, 3))
                            keys_out(t, tile0, 2)
                            if t < TILES - 1:
                                exps(t + 1, tile0, (0,))
                    strip_walk(act, st, step)
                    for t in (TILES - 2, TILES - 1):
                        rb_out(t, act.snap(st * TILES))
            act.wait_ge(s["f_in"], 48)
            for raw, w in ((rwraw, RWs), (f1raw, W1), (f2raw, W2)):
                A(flat(w, 0), raw, ACT.Copy, scale=WS).then_inc(s["fhi"], 1)
            act.wait_ge(s["b2z"], 1)
            act.wait_ge(s["b2_in"], 48)
            for j in range(3):
                last = A(B2[DH * j:DH * j + EXPERTS, :], b2raw[DH * j:DH * j + EXPERTS, :], ACT.Copy, scale=WS)
            last.then_inc(s["b2s"], 1)

            def router(img):
                act.wait_ge(s["ex_in"], img + 1)
                A(EX, EX, ACT.Exp).then_inc(s["ex_out"], 1)

            router(0)
            deviation(IMAGES + 1)
            A(cols["warm"], cols["ob"][:, 0:1], ACT.Gelu)
            with act.Fori(0, IMAGES) as img:
                act.wait_ge(s["y_mm"], img * (STRIPS * KC) + Y_CREDIT)
                act.wait_ge(s["ct_mm"], img + 1)
                for q in range(3):
                    last = nc.scalar.copy(CT[0:96, q * 2 * SN:(q + 1) * 2 * SN], ct_bank(q))
                last.then_inc(s["ct_sb"], 1)
                with act.If_eq(act.to_reg(img), 0):
                    normalised(1, IMAGES + 1)

                def hidden(i, n, a):
                    for k_ in range(KC):
                        u, unit = (3 * i + k_) % 2, n * KC + k_
                        act.wait_ge(s["h_mm"], unit + 1)
                        act.wait_ge(s["hf"], gone(unit))
                        A(GE[:, u, :], ps[:, u, 0:SN], ACT.Gelu, bias=cols["fb1"][:, k_:k_ + 1], scale=1 / WS
                          ).then_inc(s["ge"], 1)
                    act.wait_ge(s["y_mm"], n * KC + KC)
                    for k_ in range(KC):
                        u, unit = (3 * i + k_) % 2, n * KC + k_
                        act.wait_ge(s["hf"], done(unit))
                        nc.scalar.copy(HW[:, i % 2, 0, k_, :], HF[:, u, :]).then_inc(s["hh"], 1)

                expert_walk(act, img, hidden, None, lambda: router(1))

        @block.tensor
        def _(pe):
            mm = nc.tensor.matmul

            def split_product(bank, lhsT, rhs, steps=KC, finish=True):
                for k in range(steps):
                    for n, (a, b) in enumerate(((0, 0), (0, 1), (1, 0))):
                        last = mm(bank, lhsT(a, k), rhs(b, k), start=(k == 0 and n == 0),
                                  stop=(finish and k == steps - 1 and n == 2))
                return last

            def group_means(n, G):
                pe.wait_ge(s["gn_st"], n + 1)
                for j in range(KC):
                    for k in range(KC):
                        last = mm(ps[:, 7, 2 * j:2 * j + 2], G[:, k, j * P:(j + 1) * P], mv[:, k, :], start=(k == 0), stop=(k == KC - 1))
                last.then_inc(s["gn_mm"], 1)

            pe.wait_ge(s["c_in"], 16)
            group_means(0, G)
            pe.wait_ge(s["wlo"], KC)
            pe.wait_ge(s["rlo"], 1)
            for g in range(KC):
                last = split_product(ps[:, 6, REGS * g:REGS * (g + 1)], lambda a, k: WQ[:, a, k, C + g * P:C + (g + 1) * P],
                                     lambda b, k: RG[:, b, k, :])
            last.then_inc(s["kr_mm"], 1)
            pe.wait_ge(s["gn_var"], 1)
            split_product(ps[0:REGS, 7, 0:C], lambda a, k: RG[:, a, k, :], lambda b, k: WQ[:, b, k, 2 * C:3 * C]
                          ).then_inc(s["vr_mm"], 1)
            pe.wait_ge(s["id_in"], 16)

            def scores(t, m, tile0, g, h, row0, b):
                pe.wait_ge(exd[h], start(tile0 + t))
                q = QS[0:96, bass.ds(m * (2 * SN) + (h * N + t * P), P)]
                k0 = h * N + 13 * b
                span = (RR - 1) * W + RC
                if isinstance(row0, int):
                    base = KS[0:96, k0 + row0 * W:k0 + row0 * W + span]
                else:
                    base = KS[0:96, bass.ds(row0 * W + k0, span)]
                mm(S_BANK(h)[:, 0:RK], q, region_view(base), start=True, stop=True)
                mm(S_BANK(h)[:, RK:KEYS], q, KRS[0:96, h, :, :].rearrange("p k r -> p (k r)")[:, bass.ds(g * REGS, REGS)], start=True, stop=True
                   ).then_inc(s_mm[h], 1)

            def transposes(t, tile0, h):
                pe.wait_ge(exd[h], done(tile0 + t))
                pe.wait_ge(evd[(h + 2) % 4], start(tile0 + t + (1 if h >= 2 else 0)))
                for c in range(3):
                    last = nc.tensor.transpose(T_BANK(h % 2)[0:LEN[c], c * P:(c + 1) * P], PR[:, h % 2, AT[c]:AT[c] + LEN[c]], ID[:, :])
                last.then_inc(trd[h], 1)

            def values(t, tile0, pair0, c):
                p = t % 2
                if c == 0:
                    values_ready(t, tile0, pair0)
                for h in range(HEADS):
                    mm(O_BANK(p)[DH * h:DH * (h + 1), 0:P], VR[0:LEN[c], p, c, DH * h:DH * (h + 1)],
                       PT[0:LEN[c], p, h, c * P:(c + 1) * P], start=(c == 0), stop=(c == 2))
                if c == 2:
                    pe.wait_ge(s["rx"], tile0 + t + 1)
                    nc.tensor.transpose(O_BANK(p)[:, P:2 * P], RX[:, p, :], ID[:, :]).then_inc(s["pv"], 1)

            def values_ready(t, tile0, pair0):
                p = t % 2
                for h in range(HEADS):
                    pe.wait_ge(evd[h], done(tile0 + t))
                pe.wait_ge(v_in[p], start((pair0 + t // 2 + 1) * 48))
                pe.wait_ge(s["norm"], gone(tile0 + t))

            with pe.Fori(0, IMAGES) as img:
                with pe.Fori(0, KC) as g:
                    st = pe.snap(img * KC + g)

                    def project(m, i, last=False):
                        n = pe.snap(st * STRIPS + m * 2 + i)
                        pe.wait_ge(s["op_done"], st * STRIPS + (1 + i))
                        if i == 0:
                            pe.wait_ge(s["gn_lo"], img * LO_P + m * 2 + 2)
                            pe.wait_ge(s["gn_lo_v"], img * LO_V + m + 1)
                        x_ = lambda b, k: xh(img, b, k, m * (2 * SN) + i * SN, SN)
                        pe.wait_ge(s["q_lo"], gone(n))
                        split_product(ps[:, 3 * i, 0:SN], lambda a, k: WQ[:, a, k, bass.ds(g * P, P)], x_).then_inc(s["q_mm"], 1)
                        pe.wait_ge(s["k_lo"], gone(n))
                        split_product(ps[:, 3 * i + 1, 0:SN], lambda a, k: WQ[:, a, k, bass.ds(g * P + C, P)],
                                      lambda b, k: raster(x_(b, k))).then_inc(s["k_mm"], 1)
                        if last:
                            before = pe.snap(st * STRIPS + (STRIPS - 1 + CREDIT))
                            for name in ("q_lo", "k_lo", "v_sb"):
                                pe.wait_ge(s[name], before)
                            for name in ("q_in", "k_in"):
                                pe.wait_ge(s[name], st * (3 * 48) + (48 + CREDIT))
                            pe.wait_ge(s["krs_in"], 48)
                            for h in range(3):
                                scores(0, 0, pe.snap(st * TILES), g, h, 0, 0)
                        pe.wait_ge(s["v_sb"], gone(n))
                        for b_ in range(TPS):
                            done_ = split_product(ps[:, 3 * i + 2, P * b_:P * (b_ + 1)],
                                                  lambda a, k: xh(img, a, k, m * (2 * SN) + (i * SN + b_ * P), P),
                                                  lambda b, k: WQ[:, b, k, bass.ds(g * P + 2 * C, P)])
                        done_.then_inc(s["v_mm"], 1)
                        if last:
                            pe.wait_ge(s["q_lo"], done(n))
                            scores(0, 0, pe.snap(st * TILES), g, 3, 0, 0)

                    with pe.Fori(0, STRIPS // 2 - 1) as m:
                        project(m, 0)
                        project(m, 1)
                    with pe.If_eq(pe.to_reg(g), 1):
                        counted(pe, s["c2_in"], img * 16 + 16, 16)
                        group_means(pe.snap(img + 1), G)
                    project(STRIPS // 2 - 1, 0)
                    project(STRIPS // 2 - 1, 1, last=True)
                    strips = pe.snap(st * STRIPS + STRIPS + CREDIT)
                    for name in ("k_lo", "v_sb"):
                        pe.wait_ge(s[name], strips)
                    for name in ("q_in", "k_in"):
                        pe.wait_ge(s[name], st * (3 * 48) + (2 * 48 + CREDIT))
                    pe.wait_ge(s["wolo"], 1)
                    pe.wait_ge(s["vreg_in"], st * 32 + 32)
                    pe.wait_ge(s["kpad"], 1)
                    def step(i, m, tile0, pair0):
                        for b in range(TPS):
                            t = 3 * i + b
                            nxt = None
                            if t < TILES - 1:
                                a1 = i + (b + 1) // TPS
                                if a1 == 0 or a1 == 5:
                                    row0 = 0 if a1 == 0 else LAST0
                                else:
                                    row0 = pe.snap(m * (2 * TR) + (a1 * TR - 3)) if not isinstance(m, int) else a1 * TR - 3
                                nxt = (row0, (b + 1) % TPS)
                            if i == 2 and b == 0:
                                for name in ("q_in", "k_in"):
                                    pe.wait_ge(s[name], st * (3 * 48) + (3 * 48 + CREDIT))
                            for h in range(HEADS):
                                transposes(t, tile0, h)
                                if nxt:
                                    scores(t + 1, m, tile0, g, h, *nxt)
                                if h and t:
                                    values(t - 1, tile0, pair0, h - 1)
                    strip_walk(pe, st, step)

                    def output(a):
                        pe.wait_ge(s["osplit"], st * TILES + ((a + 1) * TPS + CREDIT))
                        pe.wait_ge(s["op_done"], gone(st * STRIPS + a))
                        for j in range(KC):
                            last = split_product(ps[:, 3 * (a % 2) + j, 0:SN],
                                                 lambda a, k: WO[:, a, :, :].rearrange("p k n -> p (k n)")[:, bass.ds(g * C + j * P, P)],
                                                 lambda b, k: OS[:, b * N + a * SN:b * N + (a + 1) * SN], steps=1)
                        last.then_inc(s["op_mm"], 1)

                    output(0)
                    for c in range(3):
                        values(TILES - 1, pe.snap(st * TILES), pe.snap(st * (TILES // 2)), c)
                    for a in range(1, STRIPS):
                        output(a)
            pe.wait_ge(s["flo"], 1)
            pe.wait_ge(s["op_done"], STAGES * STRIPS + CREDIT)

            def logits(img):
                pe.wait_ge(s["gn_lo"], (img + IMAGES + 1) * LO_P)
                pe.wait_ge(s["gn_lo_v"], (img + IMAGES + 1) * LO_V)
                for q in range(TILES // 6):
                    for t in range(6):
                        at = (6 * q + t) * (2 * EXPERTS)
                        for k in range(KC):
                            mm(ps[:, 5, at:at + 2 * EXPERTS], xh(img, 0, k, q * (6 * P) + t * P, P), RWs[:, :, k, :],
                               start=(k == 0), stop=False)
                            last = mm(ps[:, 5, at:at + EXPERTS], xh(img, 1, k, q * (6 * P) + t * P, P), RWs[:, 0, k, :],
                                      start=False, stop=(k == KC - 1))
                    last.then_inc(s["lg_mm"], 1)

            logits(0)
            pe.wait_ge(s["c2_in"], (IMAGES + 1) * 16)
            group_means(IMAGES + 1, G2)
            pe.wait_ge(s["flo"], 4)
            pe.wait_ge(s["moe_in"], 48)
            pe.wait_ge(s["gn_var"], IMAGES + 2)
            with pe.Fori(0, IMAGES) as img:
                pe.wait_ge(s["comb"], img + 1)
                pe.wait_ge(s["hf"], img * (STRIPS * KC) + CREDIT)
                for t in range(TILES):
                    last = nc.tensor.transpose(ct_bank(t // 6)[:, t % 6 * P:(t % 6 + 1) * P], CS[:, t, :], ID16)
                last.then_inc(s["ct_mm"], 1)
                pe.wait_ge(s["ct_sb"], img + 1)

                def hidden(i, n, a):
                    a_ = a
                    for k_ in range(KC):
                        u = (3 * i + k_) % 2
                        pe.wait_ge(s["ge"], gone(n * KC + k_))
                        split_product(ps[:, u, 0:SN], lambda a, k: W1[:, a, k, k_ * P:(k_ + 1) * P],
                                      lambda b, k: xh(img, b, k, a_ * SN, SN)).then_inc(s["h_mm"], 1)
                        if k_ == 0:
                            pe.wait_ge(s["hf"], n * KC + CREDIT)
                            for j in range(KC):
                                last = mm(ps[:, 2 + j, 0:SN], PICK[0:96, j * P:(j + 1) * P], CT[0:96, bass.ds(a * SN, SN)],
                                          start=True, stop=True)
                            last.then_inc(s["cb_mm"], 1)

                def result(i, n, a):
                    pe.wait_ge(s["hl"], n * KC + KC + CREDIT)
                    pe.wait_ge(s["hh"], n * KC + KC)
                    for j in range(KC):
                        bank = ps[:, 6 + (3 * i + j) % 2, 0:SN]
                        pe.wait_ge(s["y_done"], gone(n * KC + j))
                        split_product(bank, lambda a, k: W2[:, a, k, j * P:(j + 1) * P],
                                      lambda b, k: HW[:, i % 2, b, k, :], finish=False)
                        mm(bank, B2[0:96, j * P:(j + 1) * P], CT[0:96, bass.ds(a * SN, SN)], start=False, stop=True).then_inc(s["y_mm"], 1)

                expert_walk(pe, img, hidden, result, lambda: logits(1))


def tile_masks():
    import numpy as np

    def near(size, tile, region, first, start):
        q = first + np.arange(tile)
        w = np.clip(q - WIN // 2, 0, size - WIN)[:, None]
        k = start + np.arange(region)[None, :]
        return (k >= w) & (k < w + WIN)

    rows = [near(H, TR, RR, 0, 0), near(H, TR, RR, TR, TR - 3), near(H, TR, RR, H - TR, LAST0)]
    cols = [near(W, TC, RC, TC * b, 13 * b) for b in range(TPS)]
    out = np.zeros((9, P, KEYS), np.float32)
    for a in range(3):
        for b in range(3):
            ok = rows[a][:, None, :, None] & cols[b][None, :, None, :]
            out[3 * a + b, :, :RK] = np.where(ok.reshape(P, RK), 0.0, -1e30)
    return (out.view(np.uint32) >> 16).astype(np.uint16)


def kernel(x, L0_conv_registers, L0_conv_qkv_w, L0_conv_qkv_b, L0_conv_out_w, L0_conv_out_b, L1_conv_router_w,
           L1_conv_router_b, L1_conv_fc1_w, L1_conv_fc1_b, L1_conv_fc2_w, L1_conv_fc2_b):
    import numpy as np
    import concourse.bacc as bacc
    from concourse.bass_utils import run_bass_kernel_spmd

    def rows(w):
        w = np.asarray(w)
        return np.ascontiguousarray(w.reshape(-1, P, w.shape[-1]).transpose(1, 0, 2))

    def flat(w):
        w = rows(w)
        return w.reshape(P, -1)

    def column(b):
        return np.ascontiguousarray(np.asarray(b).reshape(-1, P).T)

    x = np.asarray(x)
    xc = x.reshape(IMAGES, STRIPS, TR, TPS, TC, KC, P).transpose(0, 6, 5, 1, 3, 2, 4).reshape(IMAGES, P, KC, N)
    qkv_b = np.asarray(L0_conv_qkv_b)
    group = np.arange(C) // (C // GROUPS)
    gmat = (group[:, None] == group[None, :]).astype(np.float32) / np.float32(C // GROUPS)
    tri = np.broadcast_to(np.tril(np.ones((EXPERTS, EXPERTS), np.float32), -1).reshape(1, -1), (P, EXPERTS ** 2))
    pick = np.zeros((96, C), np.float16)
    for row in (0, 32):
        for e in range(EXPERTS):
            pick[row + e, e * HID:(e + 1) * HID] = 1
    arrays = {
        "x": np.ascontiguousarray(xc),
        "wqkv": flat(np.asarray(L0_conv_qkv_w).T), "wo": flat(np.asarray(L0_conv_out_w).T),
        "fc1": flat(np.asarray(L1_conv_fc1_w).reshape(EXPERTS * HID, C).T),
        "fc2": flat(np.asarray(L1_conv_fc2_w).transpose(0, 2, 1).reshape(EXPERTS * HID, C)),
        "rw": flat(np.asarray(L1_conv_router_w).T), "regs": flat(np.asarray(L0_conv_registers).T),
        "qkb": column(qkv_b[:2 * C]), "bv": np.ascontiguousarray(qkv_b[2 * C:]), "ob": column(L0_conv_out_b),
        "fb1": column(np.asarray(L1_conv_fc1_b).reshape(-1)), "fb2": np.ascontiguousarray(L1_conv_fc2_b),
        "rb": np.ascontiguousarray(L1_conv_router_b), "masks": tile_masks(),
        "gmat": rows(gmat), "ident": np.eye(P, dtype=np.float32), "ident16": np.eye(P, dtype=np.float16),
        "tri": np.ascontiguousarray(tri), "pick": pick,
    }
    nc = bacc.Bacc("TRN2", target_bir_lowering=False, num_devices=1)
    aps = {n: nc.dram_tensor(f"in_{n}", a.shape, mybir.dt.from_np(a.dtype), kind="ExternalInput").ap() for n, a in arrays.items()}
    out = nc.dram_tensor("out", (IMAGES, P, KC, N), F32, kind="ExternalOutput").ap()
    build(nc, out=out, **aps)
    r = run_bass_kernel_spmd(nc, [{f"in_{n}": a for n, a in arrays.items()}], core_ids=[0])
    y = np.asarray(r.results[0]["out"])
    return np.ascontiguousarray(
        y.reshape(IMAGES, P, KC, STRIPS, TPS, TR, TC).transpose(0, 3, 5, 4, 6, 2, 1).reshape(IMAGES, H, W, C))
```
